# Optimizing a Trainium2 kernel written in Bass

```python
import numpy as np
import jax
import jax.numpy as jnp

def _softmax(x, axis=-1):
    return jax.nn.softmax(x, axis=axis)

def _gelu(x):
    return jax.nn.gelu(x, approximate=True)

def _silu(x):
    return jax.nn.silu(x)

def _sigmoid(x):
    return jax.nn.sigmoid(x)

def _layernorm(x, axis=-1, eps=1e-05):
    m = jnp.mean(x, axis=axis, keepdims=True)
    v = jnp.var(x, axis=axis, keepdims=True)
    return (x - m) / jnp.sqrt(v + eps)

def _scatter_add(tgt, idx, src, axis=0):
    return tgt.at[idx].add(src)

def _segment_sum(src, seg, n):
    return jax.ops.segment_sum(src, seg, n)
kernel_name = 'mk_perceiver_d1_seqx_r2_0a252a'

def setup_inputs(seed: int=0):
    np.random.seed(seed)
    _w = jnp.asarray

    def _rec_inputs():
        import jax
        import jax.numpy as jnp
        _rk = jax.random.key(seed)
        x = -0.0003929 + 0.9999 * jax.random.normal(jax.random.fold_in(_rk, 1), (1, 512, 1024), jnp.float32)
        _lenS = 512 - jax.random.randint(jax.random.fold_in(_rk, 7), (1,), 0, max(1, 512 // 4) + 1, jnp.int32)
        _lenS2 = 8192 - jax.random.randint(jax.random.fold_in(_rk, 8), (1,), 0, max(1, 8192 // 4) + 1, jnp.int32)
        _ctx_2048P = jax.random.normal(jax.random.fold_in(_rk, 11), (1, 16, 1024), jnp.float32)
        _ctx_2048c = jax.random.dirichlet(jax.random.fold_in(_rk, 511), 0.3 * jnp.ones((16,), jnp.float32), (1, 8192))
        _ctx_2048t = jnp.einsum('bsk,bkd->bsd', _ctx_2048c, _ctx_2048P)
        _ctx_2048t = _ctx_2048t * jax.lax.rsqrt(jnp.mean(jnp.square(_ctx_2048t)) + 1e-12) * 0.953939
        ctx_2048 = -0.000514642 + 1.00011 * (_ctx_2048t + 0.3 * jax.random.normal(jax.random.fold_in(_rk, 611), (1, 8192, 1024), jnp.float32))
        return (x, ctx_2048)
    x, ctx_2048 = _rec_inputs()

    def _L0_xattn_setup():
        import jax, jax.numpy as jnp
        import numpy as np
        DIM = 1024
        NHEADS = 32
        HEAD_DIM = DIM // NHEADS
        EPS = 1e-06

        def _rmsnorm(t):
            return t * jax.lax.rsqrt(jnp.mean(t * t, axis=-1, keepdims=True) + EPS)
        key = jax.random.key(seed)
        kx, kc, kq, kk, kv = jax.random.split(key, 5)
        x = jax.random.normal(kx, (2, 2048, DIM), dtype=jnp.float32)
        context = jax.random.normal(kc, (2, 256, DIM), dtype=jnp.float32)
        std = 0.02
        Wq = jax.random.normal(kq, (DIM, DIM), dtype=jnp.float32) * std
        Wk = jax.random.normal(kk, (DIM, DIM), dtype=jnp.float32) * std
        Wv = jax.random.normal(kv, (DIM, DIM), dtype=jnp.float32) * std
        return {'x': x, 'context': context, 'Wq': Wq, 'Wk': Wk, 'Wv': Wv}
    _L0_xattn_all = _L0_xattn_setup()
    _L0_xattn_in = {k: v for k, v in _L0_xattn_all.items() if k in ('Wq', 'Wk', 'Wv')}
    del _L0_xattn_all

    def _L0_attn_setup():
        import jax, jax.numpy as jnp
        import numpy as np
        N_HEAD = 16
        N_EMBD = 1024
        HEAD_DIM = N_EMBD // N_HEAD
        key = jax.random.key(seed)
        kx, kqkv, kp = jax.random.split(key, 3)
        B, S = (2, 1024)
        x = jax.random.normal(kx, (B, S, N_EMBD), dtype=jnp.float32)
        scale = 1.0 / np.sqrt(N_EMBD)
        Wqkv = jax.random.uniform(kqkv, (3 * N_EMBD, N_EMBD), dtype=jnp.float32, minval=-scale, maxval=scale)
        Wproj = jax.random.uniform(kp, (N_EMBD, N_EMBD), dtype=jnp.float32, minval=-scale, maxval=scale)
        return {'x': x, 'Wqkv': Wqkv, 'Wproj': Wproj}
    _L0_attn_all = _L0_attn_setup()
    _L0_attn_in = {k: v for k, v in _L0_attn_all.items() if k in ('Wqkv', 'Wproj')}
    del _L0_attn_all

    def _L0_ffn_setup():
        import jax, jax.numpy as jnp
        import numpy as np
        DIM = 1024
        HID = 2816
        ZERO_POINT = 128.0

        def _qlinear(x, wq, scale):
            W = (wq.astype(jnp.float32) - ZERO_POINT) * scale[:, None]
            return jnp.einsum('bsd,hd->bsh', x, W)
        key = jax.random.key(seed)
        ks = jax.random.split(key, 7)
        B, S = (4, 1024)
        sg = jax.random.uniform(ks[1], (HID,)) * (0.02 / np.sqrt(DIM)) + 0.0001
        su = jax.random.uniform(ks[3], (HID,)) * (0.02 / np.sqrt(DIM)) + 0.0001
        sd = jax.random.uniform(ks[5], (DIM,)) * (0.02 / np.sqrt(HID)) + 0.0001
        return {'x': jax.random.normal(ks[0], (B, S, DIM), dtype=jnp.float32), 'wq_gate': jax.random.randint(ks[2], (HID, DIM), 0, 128, dtype=jnp.int32), 's_gate': sg, 'wq_up': jax.random.randint(ks[4], (HID, DIM), 0, 128, dtype=jnp.int32), 's_up': su, 'wq_down': jax.random.randint(ks[6], (DIM, HID), 0, 128, dtype=jnp.int32), 's_down': sd}
    _L0_ffn_all = _L0_ffn_setup()
    _L0_ffn_in = {k: v for k, v in _L0_ffn_all.items() if k in ('wq_gate', 's_gate', 'wq_up', 's_up', 'wq_down', 's_down')}
    del _L0_ffn_all
    return {'x': x, 'ctx_2048': ctx_2048, 'L0_xattn_Wq': _L0_xattn_in['Wq'], 'L0_xattn_Wk': _L0_xattn_in['Wk'], 'L0_xattn_Wv': _L0_xattn_in['Wv'], 'L0_attn_Wqkv': _L0_attn_in['Wqkv'], 'L0_attn_Wproj': _L0_attn_in['Wproj'], 'L0_ffn_wq_gate': _L0_ffn_in['wq_gate'], 'L0_ffn_s_gate': _L0_ffn_in['s_gate'], 'L0_ffn_wq_up': _L0_ffn_in['wq_up'], 'L0_ffn_s_up': _L0_ffn_in['s_up'], 'L0_ffn_wq_down': _L0_ffn_in['wq_down'], 'L0_ffn_s_down': _L0_ffn_in['s_down']}

def reference(x, ctx_2048, L0_xattn_Wq, L0_xattn_Wk, L0_xattn_Wv, L0_attn_Wqkv, L0_attn_Wproj, L0_ffn_wq_gate, L0_ffn_s_gate, L0_ffn_wq_up, L0_ffn_s_up, L0_ffn_wq_down, L0_ffn_s_down):
    import jax
    import jax.numpy as jnp

    def _L0_xattn_ref(x, context, Wq, Wk, Wv):
        import jax, jax.numpy as jnp
        import numpy as np
        DIM = 1024
        NHEADS = 32
        HEAD_DIM = DIM // NHEADS
        EPS = 1e-06

        def _rmsnorm(t):
            return t * jax.lax.rsqrt(jnp.mean(t * t, axis=-1, keepdims=True) + EPS)
        b, n, _ = x.shape
        m = context.shape[1]
        q = x @ Wq.T
        k_raw = context @ Wk.T
        v_raw = context @ Wv.T
        q = q.reshape(b, n, NHEADS, HEAD_DIM).transpose(0, 2, 1, 3)
        kv = jnp.concatenate([k_raw, v_raw], axis=-1)
        kv = kv.reshape(b, m, NHEADS, HEAD_DIM, 2)
        k = kv[..., 0].transpose(0, 2, 1, 3)
        v = kv[..., 1].transpose(0, 2, 1, 3)
        q = _rmsnorm(q)
        k = _rmsnorm(k)
        scale = HEAD_DIM ** (-0.5)
        scores = jnp.einsum('bhnd,bhmd->bhnm', q, k) * scale
        attn = jax.nn.softmax(scores, axis=-1)
        out = jnp.einsum('bhnm,bhmd->bhnd', attn, v)
        return out.transpose(0, 2, 1, 3).reshape(b, n, NHEADS * HEAD_DIM)

    def _L0_attn_ref(x, Wqkv, Wproj):
        import jax, jax.numpy as jnp
        import numpy as np
        N_HEAD = 16
        N_EMBD = 1024
        HEAD_DIM = N_EMBD // N_HEAD
        B, S, E = x.shape
        qkv = x @ Wqkv.T
        q, k, v = jnp.split(qkv, 3, axis=2)
        q = q.reshape(B, S, N_HEAD, HEAD_DIM).transpose(0, 2, 1, 3)
        k = k.reshape(B, S, N_HEAD, HEAD_DIM).transpose(0, 2, 1, 3)
        v = v.reshape(B, S, N_HEAD, HEAD_DIM).transpose(0, 2, 1, 3)
        scores = jnp.einsum('bhqd,bhkd->bhqk', q, k) / jnp.sqrt(jnp.float32(HEAD_DIM))
        causal = jnp.tril(jnp.ones((S, S), dtype=bool))
        scores = jnp.where(causal[None, None, :, :], scores, -jnp.inf)
        weights = jax.nn.softmax(scores, axis=-1)
        out = jnp.einsum('bhqk,bhkd->bhqd', weights, v)
        out = out.transpose(0, 2, 1, 3).reshape(B, S, E)
        return out @ Wproj.T

    def _L0_ffn_ref(x, wq_gate, s_gate, wq_up, s_up, wq_down, s_down):
        import jax, jax.numpy as jnp
        import numpy as np
        DIM = 1024
        HID = 2816
        ZERO_POINT = 128.0

        def _qlinear(x, wq, scale):
            W = (wq.astype(jnp.float32) - ZERO_POINT) * scale[:, None]
            return jnp.einsum('bsd,hd->bsh', x, W)
        gate = _qlinear(x, wq_gate, s_gate)
        gate = jax.nn.silu(gate)
        up = _qlinear(x, wq_up, s_up)
        return _qlinear(gate * up, wq_down, s_down)
    x = x + _L0_xattn_ref(_layernorm(x, axis=-1), ctx_2048, L0_xattn_Wq, L0_xattn_Wk, L0_xattn_Wv)
    x = x + _L0_attn_ref(_layernorm(x, axis=-1), L0_attn_Wqkv, L0_attn_Wproj)
    x = x + _L0_ffn_ref(_layernorm(x, axis=-1), L0_ffn_wq_gate, L0_ffn_s_gate, L0_ffn_wq_up, L0_ffn_s_up, L0_ffn_wq_down, L0_ffn_s_down)
    return x

_drawn_inputs = setup_inputs


def setup_inputs(seed=0):
    import zlib

    import numpy as np

    out = dict(_drawn_inputs(seed))
    spreads = {}
    factors = {}
    for name, (base, spread) in spreads.items():
        noise = np.random.default_rng([zlib.crc32(name.encode()), seed]).standard_normal(out[name].shape)
        drawn = base * np.exp(spread * noise) if base else spread * noise
        out[name] = jnp.asarray(drawn.astype(out[name].dtype))
    for name, factor in factors.items():
        out[name] = (out[name] * factor).astype(out[name].dtype)
    return out
```

```python
from contextlib import ExitStack

import concourse.bass as bass
from concourse import mybir

F32 = mybir.dt.float32
F16 = mybir.dt.float16
I32 = mybir.dt.int32
ALU = mybir.AluOpType
ACT = mybir.ActivationFunctionType
AX_X = mybir.AxisListType.X

P = 128
ACT_SCALE = 64.0
W_SCALE = 1024.0
HID_SCALE = 16.0
PROD = ACT_SCALE * W_SCALE
RSQRT_MAGIC = 1597463007.0
NEWTON = 3


def build_perceiver(nc, x, ctx_t, wq_t, wkv_t, wqkv_t, wproj_t, wg_t, wu_t, wd_t, s_gate, s_up, s_down, out):
    N, D = x.shape
    CM = ctx_t.shape[3]
    M = ctx_t.shape[0] * CM
    HID = wd_t.shape[0]
    H1, DH1 = 32, D // 32
    H2, DH2 = 16, D // 16
    TT = N // P
    DC = D // P
    MT = CM // P
    NCH = M // CM
    PASSES = 2
    HP = H1 // PASSES
    GP = HP // 4
    UNITS = GP * MT * 2
    STAGES = PASSES * NCH
    HT = HID // P
    KW = HP * DH1
    assert N == 512 and D == 1024 and KW == 512 and M % CM == 0 and HID % P == 0

    with ExitStack() as stack:
        def sb(name, shape, dt):
            return stack.enter_context(nc.sbuf_tensor(name, shape, dt))

        def sem(name):
            return stack.enter_context(nc.semaphore(name))

        KB = 256
        arena = sb("arena", [P, 220 * KB], F32)

        def region(at_kb, kb, dt=F32):
            r = arena[:, int(at_kb * KB):int((at_kb + kb) * KB)]
            return r if dt == F32 else r.bitcast(dt)

        def pair(at_kb, kb, cols):
            v = region(at_kb, kb, F16).rearrange("p (s d c) -> p s d c", s=2, c=cols)
            return v[:, 0], v[:, 1]

        wkv = [pair(32 * p, 32, 2 * KW) for p in range(PASSES)]
        qT = [region(64 + 16 * p, 16, F16).rearrange("p (h n) -> p h n", n=N) for p in range(PASSES)]
        kT = [region(96 + 8 * b, 8, F16).rearrange("p (h m) -> p h m", m=CM) for b in range(2)]
        values = [region(112 + 4 * b, 4).rearrange("p (t c) -> p t c", c=KW) for b in range(2)]
        ctx_f = region(120, 8).rearrange("p (d m) -> p d m", m=CM)
        ctx_hl = [pair(128 + 8 * b, 8, CM) for b in range(2)]
        keys = [region(144 + 2 * t, 2).rearrange("p (h d) -> p h d", d=DH1) for t in range(MT)]
        key_stack = [region(148 + 4 * t, 4, F16).rearrange("p (h s d) -> p h s d", s=4, d=DH1) for t in range(MT)]
        keys_sq = [region(148 + 4 * t, 2).rearrange("p (h d) -> p h d", d=DH1) for t in range(MT)]
        probs = [region(156 + 4 * b, 4) for b in range(4)]
        prob_sum = region(172, 32)
        att = region(204, 16).rearrange("p (g n) -> p g n", n=N)
        x_a = region(166, 16).rearrange("p (t c) -> p t c", c=D)
        xa_hl = pair(182, 16, N)
        norm_a = [region(198 + 4 * b, 4) for b in range(2)]
        q_raw = [region(206 + 4 * b, 4).rearrange("p (h d) -> p h d", d=DH1) for b in range(2)]
        q_sq = region(150, 4).rearrange("p (h d) -> p h d", d=DH1)
        q_stack = [region(96 + 8 * b, 8, F16).rearrange("p (h s d) -> p h s d", s=4, d=DH1) for b in range(2)]
        wq = pair(32, 32, D)
        x1 = region(64, 16).rearrange("p (t c) -> p t c", c=D)
        wqkv = [pair(at_, 32, D) for at_ in (0, 32, 166)]
        wproj = pair(0, 32, D)
        xb_hl = pair(80, 16, N)
        norm_b = [region(128 + 4 * b, 4) for b in range(2)]
        q2T = region(96, 16).rearrange("p (c n) -> p c n", n=N)
        k2T = region(144, 16).rearrange("p (c n) -> p c n", n=N)
        v2 = region(198, 16).rearrange("p (t c) -> p t c", c=D)
        sa_p = [region(136 + 2 * b, 2) for b in range(4)]
        sa_pT = [region(32 + 8 * b, 8).rearrange("p (k n) -> p k n", n=N) for b in range(2)]
        sa_out = pair(48, 16, N)
        mask = region(164, 2)
        sa_max, sa_neg, sa_sum, sa_inv = [region(160 + 0.25 * k, 0.25) for k in range(4)]
        w_stage = [region(112 + 4 * b, 4) for b in range(4)]
        ring = [[pair(166 + 8 * r + 4 * m, 4, P) for m in range(2)] for r in range(4)]
        w_down = [pair(4 * j if j < 16 else 140 + 4 * (j - 16), 4, D) for j in range(HT)]
        hid_at = [96 + 2 * j for j in range(8)] + [128 + 2 * j for j in range(6)] + [198 + 2 * j for j in range(8)]
        hid = [pair(a, 2, N) for a in hid_at]
        s_down_b = region(214, 4)
        silu_b = [region(164, 2), region(218, 2)]
        sg = sb("sg", [P, HT], F32)
        su = sb("su", [P, HT], F32)
        slots = [region(a, 4) for a in (214, 158, 162, 120, 124, 64, 68)]

        ident = sb("ident", [P, P], F32)
        ident16 = sb("ident16", [P, P], F16)
        ones = sb("ones", [P, DH1], F32)
        bn = sb("bn", [P, 2, 6], F32)
        mv = sb("mv", [P, TT, 2], F32)
        nt_v = sb("nt_v", [P, 32], F32)
        nt_y = sb("nt_y", [P, 32], F32)
        nt_t = sb("nt_t", [P, 32], F32)
        rs_key = [sb(f"rs_key{t}", [P, HP], F32) for t in range(MT)]
        rs_q = sb("rs_q", [P, H1], F32)
        rden = region(150, 2)
        rs_ln = sb("rs_ln", [P, TT], F32)

        ps = stack.enter_context(nc.psum_tensor("ps", [P, 8, 512], F32))
        SCORES, OUTS, WORK = 0, 4, 6

        ident_ready = sem("ident_ready")
        x_loaded = [sem(f"x_loaded{t}") for t in range(TT)]
        ctx_loaded = sem("ctx_loaded")
        ctx_hi_ready = sem("ctx_hi_ready")
        ctx_split = sem("ctx_split")
        w_loaded = [sem(f"w_loaded{s}") for s in range(len(slots))]
        w_hi_ready = sem("w_hi_ready")
        w_split = sem("w_split")
        dve_step = sem("dve_step")
        normed = sem("normed")
        front_ready = sem("front_ready")
        ln_hi_ready = sem("ln_hi_ready")
        front_free = sem("front_free")
        work_ready = sem("work_ready")
        work_out = sem("work_out")
        q_normed = sem("q_normed")
        q_hi = sem("q_hi")
        q_stacked = sem("q_stacked")
        key_sq_ready = sem("key_sq_ready")
        key_rs_ready = sem("key_rs_ready")
        key_normed = sem("key_normed")
        key_hi = sem("key_hi")
        key_stacked = sem("key_stacked")
        scores_ready = sem("scores_ready")
        probs_ready = sem("probs_ready")
        probs_summed = sem("probs_summed")
        pv_done = sem("pv_done")
        outs_added = sem("outs_added")
        att_ready = sem("att_ready")

        x_again = sem("x_again")
        sa_scores = sem("sa_scores")
        sa_masked = sem("sa_masked")
        sa_exp = sem("sa_exp")
        sa_norm = sem("sa_norm")
        sa_turned = sem("sa_turned")
        sa_turned_out = sem("sa_turned_out")
        sa_pv = sem("sa_pv")
        sa_out_hi = sem("sa_out_hi")
        sa_out_split = sem("sa_out_split")
        mask_ready = sem("mask_ready")
        proj_ready = sem("proj_ready")
        proj_added = sem("proj_added")
        f_loaded = [sem(f"f_loaded{b}") for b in range(4)]
        scales_loaded = sem("scales_loaded")
        scales_ready = sem("scales_ready")
        f_value = sem("f_value")
        f_hi = sem("f_hi")
        f_split = sem("f_split")
        gu_ready = sem("gu_ready")
        silu_ready = sem("silu_ready")
        hid_ready = sem("hid_ready")
        hid_hi = sem("hid_hi")
        hid_split = sem("hid_split")
        down_ready = sem("down_ready")
        down_scaled = sem("down_scaled")
        down_out = sem("down_out")
        stored = sem("stored")

        work_no = {}
        q_order = []
        for t in range(TT + 1):
            if t < TT:
                q_order += [("q", t, h) for h in range(2)]
            if t >= 1:
                q_order += [("qt", t - 1, b) for b in range(H1 // 8)]
        for n, task in enumerate(q_order):
            work_no[task] = n
        W0 = len(q_order)
        TASKS = [("K", 0, 0), ("K", 1, 0), ("T", 0, 0), ("T", 0, 1), ("V", 0, 0), ("T", 1, 0), ("T", 1, 1), ("V", 1, 0)]
        TASK_BANK = [0, 1, 1, 1, 0, 0, 0, 1]
        TASK_FREE = [-1, 0, 2, 3, 1, 5, 6, 4]
        NT = len(TASKS)
        products = [(TASKS.index((kind, t, 0)), i, i == 3 * DC - 1) for kind in "KV" for t in range(MT) for i in range(3 * DC)]
        PER_STEP = len(products) // UNITS
        T_STEPS = {9: ("T", 0, 0), 10: ("T", 0, 1), 13: ("T", 1, 0), 14: ("T", 1, 1)}
        per_step = [products[u * PER_STEP:(u + 1) * PER_STEP] +
                    [(TASKS.index(T_STEPS[u]), i, i == 7) for i in range(8) if u in T_STEPS] for u in range(UNITS)]
        task_end = {it[0]: u for u, its in enumerate(per_step) for it in its if it[2]}
        assert sorted(task_end, key=task_end.get) == list(range(NT))

        FRONT_LN1 = 0
        FRONT_DEN = FRONT_LN1 + 2 * TT
        FRONT_BACK = FRONT_DEN + PASSES * GP
        FRONT_LN2 = FRONT_BACK + 2 * TT
        FRONT_LN3 = FRONT_LN2 + 2 * TT

        w_jobs = []
        for d in range(DC):
            w_jobs.append((wq_t[d * P:(d + 1) * P, :], wq[0][:, d], wq[1][:, d], d % 3))
        for p in range(PASSES):
            for d in range(DC):
                w_jobs.append((wkv_t[d * P:(d + 1) * P, p * 1024:(p + 1) * 1024], wkv[p][0][:, d], wkv[p][1][:, d],
                               len(w_jobs) % 3))
        W_Q, W_KV, W_KV2, W_END = 0, DC, 2 * DC, 3 * DC
        W_SA = W_END
        for part in range(3):
            for d in range(DC):
                w_jobs.append((wqkv_t[d * P:(d + 1) * P, part * D:(part + 1) * D], wqkv[part][0][:, d],
                               wqkv[part][1][:, d], 5 + d % 2 if part == 0 else (3, 4, 0)[(len(w_jobs) - W_SA - DC) % 3]))
        W_PROJ = len(w_jobs)
        for d in range(DC):
            w_jobs.append((wproj_t[d * P:(d + 1) * P, :], wproj[0][:, d], wproj[1][:, d], (3, 4, 0)[(len(w_jobs) - W_SA - DC) % 3]))
        slot_use = []
        for j, job in enumerate(w_jobs):
            slot_use.append(sum(1 for k in w_jobs[:j] if k[3] == job[3]))
        slot_before = [max([k for k in range(j) if w_jobs[k][3] == w_jobs[j][3]], default=None) for j in range(len(w_jobs))]

        def unit(u):
            g, rest = divmod(u, 2 * MT)
            t, pr = divmod(rest, 2)
            return g, t, 4 * g + 2 * pr

        ctx_v = ctx_t.rearrange("c p d m -> c p (d m)")
        x_v = x.rearrange("(t p) c -> t p c", p=P)

        def at_least(eng, s, n):
            if not isinstance(n, int) or n > 0:
                eng.wait_ge(s, n)

        def stages(eng, emit):
            for p in range(PASSES):
                base = p * NCH
                emit(base, 0, p)
                emit(base + 1, 1, p)
                with eng.Fori(0, (NCH - 4) // 2) as i:
                    for b in range(2):
                        emit(i * 2 + (base + 2 + b), b, p)
                emit(base + NCH - 2, 0, p)
                emit(base + NCH - 1, 1, p)

        def last_of_pass(s):
            return isinstance(s, int) and s % NCH == NCH - 1

        def first_of_pass(s):
            return isinstance(s, int) and s % NCH == 0

        def pass_of_next(s, p):
            return p + 1 if last_of_pass(s) else p

        W_STEPS = (4, 7, 10, 13)

        W1 = W0 + NT * STAGES
        SA_UNITS = H2 * TT
        SA_LAG = 3

        f_jobs = [(m, j) for j in range(4) for m in ("gate", "up")]
        for j in range(HT):
            f_jobs.append(("down", j))
            if j + 4 < HT:
                f_jobs += [("gate", j + 4), ("up", j + 4)]
        f_no = {job: n for n, job in enumerate(f_jobs)}
        F_AHEAD = 8
        CODE_SCALE = 2.0 ** -14
        GU_SCALE = 1.0 / (CODE_SCALE * ACT_SCALE)

        def f_dest(job):
            m, j = job
            if m == "down":
                return [v.rearrange("p a c -> p (a c)") for v in w_down[j]]
            return [v.rearrange("p a c -> p (a c)") for v in ring[j % 4][m == "up"]]

        def f_turn(j):
            return [f_no[job] for job in [("down", j), ("gate", j + 4), ("up", j + 4)] if job in f_no]

        def after_sp(sp, load_w):
            sp.wait_ge(ctx_split, STAGES)
            for j in range(W_SA + DC, len(w_jobs)):
                if j == W_SA + DC + 2:
                    sp.wait_ge(front_ready, FRONT_LN2)
                load_w(j)
            sp.dma_start(sg[:, :], s_gate).then_inc(scales_loaded, 16)
            sp.dma_start(su[:, :], s_up).then_inc(scales_loaded, 16)
            sp.wait_ge(w_split, len(w_jobs))
            sp.dma_start(s_down_b, s_down.to_broadcast([P, D])).then_inc(scales_loaded, 16)
            for n, (m, j) in enumerate(f_jobs):
                src = {"gate": lambda: wg_t[j].rearrange("p d c -> p (d c)"),
                       "up": lambda: wu_t[j].rearrange("p d c -> p (d c)"),
                       "down": lambda: wd_t[j * P:(j + 1) * P, :]}[m]()
                at_least(sp, f_split, n - 3)
                sp.dma_start(w_stage[n % 4].bitcast(I32), src).then_inc(f_loaded[n % 4], 16)
            for t in range(TT):
                for h in range(2):
                    sp.wait_ge(down_out, 2 * t + h + 1)
                    sp.dma_start(out[t * P:(t + 1) * P, 512 * h:512 * h + 512], x1[:, t, 512 * h:512 * h + 512])\
                        .then_inc(stored, 16)
            sp.wait_ge(stored, 16 * 2 * TT)

        def after_pool(pool):
            pool.wait_ge(att_ready, PASSES * GP)
            nc.gpsimd.memset(mask, 0.0).then_inc(mask_ready, 1)
            pool.wait_ge(mask_ready, 1)
            diagonal = mask[:, 3 * P:4 * P]
            nc.gpsimd.affine_select(out=diagonal, in_=diagonal, compare_op=ALU.is_ge, fill=-1e30, base=0,
                                    pattern=[[-1, P]], channel_multiplier=1).then_inc(mask_ready, 1)
            for j in range(HT):
                pool.wait_ge(hid_hi, j + 1)
                nc.gpsimd.tensor_tensor(hid[j][1][:, 0], silu_b[j % 2], hid[j][0][:, 0], ALU.subtract).then_inc(hid_split, 1)

        def after_act(act, split_w, ln_hi):
            for k in range(2 * TT):
                ln_hi(k // 2, k % 2, FRONT_LN2 + k, 1, xb_hl[0])
            for n in range(3 * DC):
                part, c = divmod(n, DC)
                act.wait_ge(work_ready, W1 + n + 1)
                dst = (q2T[:, c], k2T[:, c], v2[:, c // 2, 512 * (c % 2):512 * (c % 2) + 512])[part]
                nc.scalar.activation(dst, ps[:, WORK + n % 2, :], ACT.Copy, scale=1.0 / PROD).then_inc(work_out, 1)
                split_w(W_SA + DC + n)
            for k in range(SA_UNITS + 9):
                if k < SA_UNITS:
                    L = (k % TT + 1) * P
                    act.wait_ge(sa_masked, k + 1)
                    at_least(act, sa_turned, k - 3)
                    nc.scalar.activation(sa_p[k % 4][:, 0:L], ps[:, k % 4, 0:L], ACT.Exp, bias=sa_neg[:, k:k + 1],
                                         scale=DH2 ** -0.5, accum_out=sa_sum[:, k:k + 1]).then_inc(sa_exp, 1)
                m = k - SA_LAG
                if 0 <= m < SA_UNITS:
                    h, t = divmod(m, TT)
                    act.wait_ge(sa_turned, m + 1)
                    at_least(act, sa_pv, h - 1)
                    nc.scalar.activation(sa_pT[h % 2][:, 0:t + 1, t * P:(t + 1) * P],
                                         ps[:, WORK + m % 2, 0:(t + 1) * P].rearrange("p (k n) -> p k n", n=P),
                                         ACT.Copy).then_inc(sa_turned_out, 1)
                if k >= 16 and k % 8 == 0 or k == SA_UNITS + 8:
                    i = k // 8 - 2
                    act.wait_ge(sa_pv, 2 * i + 2)
                    nc.scalar.activation(sa_out[0][:, i], ps[:, OUTS + i % 2, :], ACT.Copy,
                                         scale=ACT_SCALE).then_inc(sa_out_hi, 1)

            def f_high(n):
                act.wait_ge(f_value, n + 1)
                nc.scalar.activation(f_dest(f_jobs[n])[0], w_stage[n % 4], ACT.Copy).then_inc(f_hi, 1)

            for n in range(F_AHEAD):
                f_high(n)
            for k in range(2 * TT):
                ln_hi(k // 2, k % 2, FRONT_LN3 + k, 2, xb_hl[0])
            act.wait_ge(scales_ready, 1)
            for j in range(HT + 1):
                if j < HT:
                    act.wait_ge(gu_ready, 2 * j + 1)
                    at_least(act, hid_split, j - 1)
                    nc.scalar.activation(silu_b[j % 2], ps[:, (WORK, OUTS)[j % 2], :], ACT.Silu,
                                         scale=sg[:, j:j + 1]).then_inc(silu_ready, 1)
                if j >= 1:
                    act.wait_ge(hid_ready, j)
                    nc.scalar.activation(hid[j - 1][0][:, 0], silu_b[(j - 1) % 2], ACT.Copy).then_inc(hid_hi, 1)
                if j < HT:
                    act.wait_ge(gu_ready, 2 * j + 2)
                    for n in f_turn(j):
                        f_high(n)

        def after_dve(dve, step, split_w, layernorm):
            dve.wait_ge(x_again, 16)
            for k in range(2 * TT):
                t, q = divmod(k, 2)
                dve.wait_ge(front_ready, FRONT_BACK + k + 1)
                xs = x1[:, t, 512 * q:512 * q + 512]
                nc.vector.tensor_tensor(xs, ps[:, (FRONT_BACK + k) % 4, :], xs, ALU.add).then_inc(front_free, 1)
            layernorm(1, x1, norm_b, xb_hl, FRONT_LN2, lambda t: dve.wait_ge(front_free, FRONT_BACK + 2 * t + 2))
            for n in range(3 * DC):
                split_w(W_SA + DC + n)
            dve.wait_ge(mask_ready, 2)
            for k in range(SA_UNITS + 9):
                if k < SA_UNITS:
                    L = (k % TT + 1) * P
                    s_ = ps[:, k % 4, 0:L]
                    dve.wait_ge(sa_scores, k + 1)
                    step(nc.vector.tensor_tensor_reduce(out=s_, in0=s_, in1=mask[:, 4 * P - L:4 * P], scale=1.0, scalar=-3e38,
                                                        op0=ALU.add, op1=ALU.max, accum_out=sa_max[:, k:k + 1]))
                    nc.vector.tensor_scalar(sa_neg[:, k:k + 1], sa_max[:, k:k + 1], -(DH2 ** -0.5), None, ALU.mult)\
                        .then_inc(sa_masked, 1)
                if 1 <= k <= SA_UNITS:
                    m = k - 1
                    L = (m % TT + 1) * P
                    dve.wait_ge(sa_exp, m + 1)
                    step(nc.vector.reciprocal(sa_inv[:, m:m + 1], sa_sum[:, m:m + 1]))
                    nc.vector.tensor_scalar(sa_p[m % 4][:, 0:L], sa_p[m % 4][:, 0:L], sa_inv[:, m:m + 1], None,
                                            ALU.mult).then_inc(sa_norm, 1)
                if k >= 16 and k % 8 == 0 or k == SA_UNITS + 8:
                    i = k // 8 - 2
                    dve.wait_ge(sa_out_hi, i + 1)
                    nc.vector.scalar_tensor_tensor(sa_out[1][:, i], ps[:, OUTS + i % 2, :], ACT_SCALE, sa_out[0][:, i],
                                                   ALU.mult, ALU.subtract).then_inc(sa_out_split, 1)

            def f_float(n):
                dve.wait_ge(f_loaded[n % 4], 16 * (n // 4 + 1))
                nc.vector.tensor_scalar(w_stage[n % 4], w_stage[n % 4].bitcast(I32), -128.0, CODE_SCALE, ALU.add,
                                        ALU.mult).then_inc(f_value, 1)

            def f_low(n):
                hi, lo = f_dest(f_jobs[n])
                dve.wait_ge(f_hi, n + 1)
                nc.vector.tensor_tensor(lo, w_stage[n % 4], hi, ALU.subtract).then_inc(f_split, 1)

            dve.wait_ge(scales_loaded, 48)
            step(nc.vector.tensor_scalar(su[:, :], su[:, :], GU_SCALE * HID_SCALE, None, ALU.mult))
            step(nc.vector.tensor_scalar(s_down_b, s_down_b, 1.0 / (CODE_SCALE * HID_SCALE), None, ALU.mult))
            nc.vector.tensor_scalar(sg[:, :], sg[:, :], GU_SCALE, None, ALU.mult).then_inc(scales_ready, 1)
            for k in range(2 * TT):
                t, h = divmod(k, 2)
                dve.wait_ge(proj_ready, k + 1)
                xs = x1[:, t, 512 * h:512 * h + 512]
                nc.vector.scalar_tensor_tensor(xs, ps[:, WORK + k % 2, :], 1.0 / PROD, xs, ALU.mult,
                                               ALU.add).then_inc(proj_added, 1)
                f_float(k)
                if k >= 1:
                    f_low(k - 1)
            f_low(F_AHEAD - 1)
            layernorm(2, x1, norm_b, xb_hl, FRONT_LN3, lambda t: dve.wait_ge(proj_added, 2 * t + 2))
            for j in range(HT):
                turn = f_turn(j)
                f_float(turn[0])
                dve.wait_ge(silu_ready, j + 1)
                dve.wait_ge(gu_ready, 2 * j + 2)
                nc.vector.scalar_tensor_tensor(silu_b[j % 2], ps[:, (WORK, OUTS)[j % 2] + 1, :], su[:, j:j + 1],
                                               silu_b[j % 2], ALU.mult, ALU.mult).then_inc(hid_ready, 1)
                for n in turn[1:]:
                    f_float(n)
                    f_low(n - 1)
                f_low(turn[-1])
            for k in range(2 * TT):
                t, h = divmod(k, 2)
                b = ps[:, k % 4, :]
                xs = x1[:, t, 512 * h:512 * h + 512]
                dve.wait_ge(down_ready, k + 1)
                nc.vector.tensor_tensor(b, b, s_down_b[:, 512 * h:512 * h + 512], ALU.mult).then_inc(down_scaled, 1)
                dve.wait_ge(down_scaled, k + 1)
                nc.vector.tensor_tensor(xs, b, xs, ALU.add).then_inc(down_out, 1)

        def after_pe(pe, transpose_tokens, split_product):
            pe.wait_ge(att_ready, PASSES * GP)
            for k in range(2 * TT):
                t, q = divmod(k, 2)
                f = FRONT_BACK + k
                pe.wait_ge(front_free, f - 3)
                for g in range(4):
                    last = nc.tensor.transpose(ps[:, f % 4, g * P:(g + 1) * P], att[:, 4 * q + g, t * P:(t + 1) * P],
                                               ident[:, :])
                last.then_inc(front_ready, 1)
            transpose_tokens(FRONT_LN2, norm_b, 1)
            pe.wait_ge(w_split, W_SA + DC)
            pe.wait_ge(front_free, FRONT_LN2 + 2 * TT)
            for n in range(3 * DC):
                part, c = divmod(n, DC)
                pe.wait_ge(work_out, W1 + n - 1)
                if c == 0 and part:
                    pe.wait_ge(w_split, W_SA + (part + 1) * DC)
                if part < 2:
                    left = [lambda d, v=v: v[:, d, c * P:(c + 1) * P] for v in wqkv[part]]
                    right = [lambda d, v=v: v[:, d, :] for v in xb_hl]
                else:
                    t, h = divmod(c, 2)
                    left = [lambda d, v=v: v[:, d, t * P:(t + 1) * P] for v in xb_hl]
                    right = [lambda d, v=v: v[:, d, 512 * h:512 * h + 512] for v in wqkv[2]]
                for i in range(3 * DC):
                    last = split_product(ps[:, WORK + n % 2, :], left, right, i, i == 3 * DC - 1)
                last.then_inc(work_ready, 1)

            pe.wait_ge(work_out, W1 + 3 * DC)
            for k in range(SA_UNITS + SA_LAG + 3):
                if k < SA_UNITS:
                    h, t = divmod(k, TT)
                    at_least(pe, sa_exp, k - 3)
                    rows = slice(64 * (h % 2), 64 * (h % 2) + 64)
                    nc.tensor.matmul(ps[:, k % 4, 0:(t + 1) * P], q2T[rows, h // 2, t * P:(t + 1) * P],
                                     k2T[rows, h // 2, 0:(t + 1) * P], start=True, stop=True).then_inc(sa_scores, 1)
                m = k - SA_LAG
                if 0 <= m < SA_UNITS:
                    t = m % TT
                    pe.wait_ge(sa_norm, m + 1)
                    at_least(pe, sa_turned_out, m - 1)
                    for c in range(t + 1):
                        last = nc.tensor.transpose(ps[:, WORK + m % 2, c * P:(c + 1) * P], sa_p[m % 4][:, c * P:(c + 1) * P],
                                                   ident[:, :])
                    last.then_inc(sa_turned, 1)
                m -= 2
                if m >= 0 and m % TT == TT - 1:
                    h = m // TT
                    pe.wait_ge(sa_turned_out, m + 1)
                    if h % 2 == 0:
                        at_least(pe, sa_out_split, h // 2 - 1)
                    for c in range(TT):
                        last = nc.tensor.matmul(ps[64 * (h % 2):64 * (h % 2) + 64, OUTS + h // 2 % 2, c * P:N],
                                                v2[:, c, h * DH2:(h + 1) * DH2], sa_pT[h % 2][:, c, c * P:N],
                                                start=(c == 0), stop=(c == TT - 1))
                    last.then_inc(sa_pv, 1)

            pe.wait_ge(w_split, len(w_jobs))
            pe.wait_ge(sa_out_split, H2 // 2)
            for k in range(2 * TT):
                t, h = divmod(k, 2)
                at_least(pe, proj_added, k - 1)
                left = [lambda d, v=v: v[:, d, t * P:(t + 1) * P] for v in sa_out]
                right = [lambda d, v=v: v[:, d, 512 * h:512 * h + 512] for v in wproj]
                for i in range(3 * DC):
                    last = split_product(ps[:, WORK + k % 2, :], left, right, i, i == 3 * DC - 1)
                last.then_inc(proj_ready, 1)

            transpose_tokens(FRONT_LN3, norm_b, 2)
            pe.wait_ge(front_free, FRONT_LN3 + 2 * TT)
            for j in range(HT):
                pe.wait_ge(f_split, f_no["up", j] + 1)
                for m in range(2):
                    at_least(pe, (silu_ready, hid_ready)[m], j - 1)
                    left = [lambda d, v=v: v[:, d, :] for v in ring[j % 4][m]]
                    right = [lambda d, v=v: v[:, d, :] for v in xb_hl]
                    for i in range(3 * DC):
                        last = split_product(ps[:, (WORK, OUTS)[j % 2] + m, :], left, right, i, i == 3 * DC - 1)
                    last.then_inc(gu_ready, 1)
            pe.wait_ge(hid_split, HT)
            pe.wait_ge(f_split, len(f_jobs))
            for k in range(2 * TT):
                t, h = divmod(k, 2)
                at_least(pe, down_out, k - 3)
                left = [lambda j, v=v: hid[j][v][:, 0, t * P:(t + 1) * P] for v in range(2)]
                right = [lambda j, v=v: w_down[j][v][:, 0, 512 * h:512 * h + 512] for v in range(2)]
                for i in range(3 * HT):
                    last = split_product(ps[:, k % 4, :], left, right, i, i == 3 * HT - 1)
                last.then_inc(down_ready, 1)

        block = stack.enter_context(nc.Block())

        @block.sync
        def _(sp):
            for t in range(TT):
                sp.dma_start(x_a[:, t], x_v[t]).then_inc(x_loaded[t], 16)

            def load_w(j):
                src, _, _, slot = w_jobs[j]
                if slot_before[j] is not None:
                    sp.wait_ge(w_split, slot_before[j] + 1)
                sp.dma_start(slots[slot], src).then_inc(w_loaded[slot], 16)

            def load_ctx(c, chunk):
                at_least(sp, ctx_split, c)
                sp.dma_start(region(120, 8), ctx_v[bass.ds(chunk, 1)].rearrange("c p x -> (c p) x"))\
                    .then_inc(ctx_loaded, 16)

            load_ctx(0, 0)
            for j in range(W_KV2):
                load_w(j)
            load_ctx(1, 1)
            for j in range(W_KV2, W_END):
                load_w(j)
            load_ctx(2, 2)
            with sp.Fori(0, NCH - 3) as i:
                load_ctx(i + 3, i + 3)
            for k in range(3):
                load_ctx(NCH + k, k)
            sp.wait_ge(scores_ready, NCH * UNITS)
            load_w(W_END)
            load_w(W_END + 1)
            load_ctx(NCH + 3, 3)
            for j in range(W_END + 2, W_SA + DC):
                load_w(j)
            sp.wait_ge(w_split, W_SA + DC)
            sp.dma_start(x1, x.rearrange("(t p) c -> p t c", p=P)).then_inc(x_again, 16)
            with sp.Fori(0, NCH - 4) as i:
                load_ctx(i + (NCH + 4), i + 4)
            after_sp(sp, load_w)

        @block.gpsimd
        def _(pool):
            nc.gpsimd.memset(ident[:, :], 0.0).then_inc(ident_ready, 1)
            nc.gpsimd.memset(ident16[:, :], 0.0).then_inc(ident_ready, 1)
            nc.gpsimd.memset(ones[:, :], 1.0).then_inc(ident_ready, 1)
            pool.wait_ge(ident_ready, 3)
            for m in (ident, ident16):
                nc.gpsimd.affine_select(out=m[:, :], in_=m[:, :], compare_op=ALU.not_equal, fill=1.0, base=0,
                                        pattern=[[-1, P]], channel_multiplier=1).then_inc(ident_ready, 1)

            def key_tile(c, t):
                n = c * MT + t
                pool.wait_ge(work_out, c * NT + (W0 + t + 1))
                nc.gpsimd.tensor_tensor(keys_sq[t], keys[t], keys[t], ALU.mult).then_inc(key_sq_ready, 1)
                pool.wait_ge(key_rs_ready, n + 1)
                nc.gpsimd.tensor_tensor(keys[t], keys[t], rs_key[t][:, :].unsqueeze(2).to_broadcast([P, HP, DH1]),
                                        ALU.mult).then_inc(key_normed, 1)
                pool.wait_ge(key_hi, n + 1)
                nc.gpsimd.tensor_tensor(key_stack[t][:, :, 1::2, :],
                                        keys[t].unsqueeze(2).to_broadcast([P, HP, 2, DH1]),
                                        key_stack[t][:, :, 0::2, :], ALU.subtract).then_inc(key_stacked, 1)

            def stage(s, b, p):
                if isinstance(s, int) and s + 1 >= STAGES:
                    return
                for t in range(MT):
                    key_tile(s + 1, t)

            for t in range(MT):
                key_tile(0, t)
            stages(pool, stage)
            after_pool(pool)

        @block.scalar
        def _(act):
            def split_w(j):
                src, hi, _, slot = w_jobs[j]
                act.wait_ge(w_loaded[slot], 16 * (slot_use[j] + 1))
                nc.scalar.activation(hi, slots[slot], ACT.Copy, scale=W_SCALE).then_inc(w_hi_ready, 1)

            def ln_hi(t, q, front, ln, hi):
                act.wait_ge(front_ready, front + 1)
                nc.scalar.activation(hi[:, 4 * q:4 * q + 4, t * P:(t + 1) * P],
                                     ps[:, front % 4, :].rearrange("p (d n) -> p d n", n=P), ACT.Copy,
                                     scale=ACT_SCALE).then_inc(ln_hi_ready, 1)

            def ctx_hi(c, b):
                act.wait_ge(ctx_loaded, (c + 1) * 16)
                nc.scalar.activation(ctx_hl[b][0], ctx_f, ACT.Copy, scale=ACT_SCALE).then_inc(ctx_hi_ready, 1)

            def copy_out(c, n, b):
                kind, t, h = TASKS[n]
                no = c * NT + (W0 + n)
                bank = WORK + TASK_BANK[n]
                act.wait_ge(work_ready, no + 1)
                if kind == "K":
                    at_least(act, key_stacked, c * MT + (t - 1))
                    nc.scalar.activation(keys[t], ps[:, bank, :].rearrange("p (h d) -> p h d", d=DH1), ACT.Copy,
                                         scale=1.0 / PROD).then_inc(work_out, 1)
                elif kind == "V":
                    nc.scalar.activation(values[b][:, t], ps[:, bank, :], ACT.Copy,
                                         scale=1.0 / PROD).then_inc(work_out, 1)
                else:
                    nc.scalar.activation(kT[b][:, 8 * h:8 * h + 8, t * P:(t + 1) * P],
                                         ps[:, bank, :].bitcast(F16).rearrange("p (h m) -> p h m", m=P),
                                         ACT.Copy).then_inc(work_out, 1)

            def key_high(c, t):
                act.wait_ge(key_normed, c * MT + (t + 1))
                nc.scalar.activation(key_stack[t][:, :, 0::2, :], keys[t].unsqueeze(2).to_broadcast([P, HP, 2, DH1]),
                                     ACT.Copy).then_inc(key_hi, 1)

            for t in range(TT):
                for q in range(2):
                    ln_hi(t, q, FRONT_LN1 + 2 * t + q, 0, xa_hl[0])
            for j in range(W_Q, W_KV):
                split_w(j)
            for task in q_order:
                kind, t, h = task
                no = work_no[task]
                act.wait_ge(work_ready, no + 1)
                bank = ps[:, WORK + no % 2, :]
                if kind == "q":
                    if t >= 2 and h == 0:
                        act.wait_ge(q_stacked, t - 1)
                    nc.scalar.activation(q_raw[t % 2][:, 16 * h:16 * h + 16], bank.rearrange("p (h d) -> p h d", d=DH1),
                                         ACT.Copy, scale=1.0 / PROD).then_inc(work_out, 1)
                    split_w(W_KV + 2 * t + h)
                    if h == 1:
                        if t == 0:
                            ctx_hi(0, 0)
                        if t == 2:
                            ctx_hi(1, 1)
                        act.wait_ge(q_normed, t + 1)
                        nc.scalar.activation(q_stack[t % 2][:, :, 0:2, :],
                                             q_raw[t % 2].unsqueeze(2).to_broadcast([P, H1, 2, DH1]),
                                             ACT.Copy).then_inc(q_hi, 1)
                else:
                    dst = qT[8 * h // HP][:, 8 * h % HP:8 * h % HP + 8, t * P:(t + 1) * P]
                    nc.scalar.activation(dst, bank.bitcast(F16).rearrange("p (h m) -> p h m", m=P),
                                         ACT.Copy).then_inc(work_out, 1)
            for n in range(NT):
                copy_out(0, n, 0)
                if n in (1, 2):
                    key_high(0, n - 1)
                split_w(W_KV2 + n)

            def stage(s, b, p):
                project = not (isinstance(s, int) and s + 1 >= STAGES)
                for u in range(UNITS):
                    n = s * UNITS + u
                    if isinstance(s, int) and s == 0 and u == 0:
                        act.wait_ge(w_split, W_END)
                    act.wait_ge(scores_ready, n + 1)
                    at_least(act, pv_done, s * (UNITS // 2) + (u // 2 - 1))
                    at_least(act, probs_summed, n - 3)
                    nc.scalar.activation(probs[u % 4], ps[:, SCORES + 2 * (u % 2):SCORES + 2 * (u % 2) + 2, :]
                                         .rearrange("p a n -> p (a n)"), ACT.Exp,
                                         scale=DH1 ** -0.5 / ACT_SCALE ** 2).then_inc(probs_ready, 1)
                    if isinstance(s, int) and s in (NCH, NCH + 1) and u in W_STEPS:
                        split_w(W_SA + (s - NCH) * 4 + W_STEPS.index(u))
                    if not project:
                        continue
                    if u == 1 and not (isinstance(s, int) and s + 2 >= STAGES):
                        ctx_hi(s + 2, b)
                    for k in range(NT):
                        if task_end[k] == u:
                            copy_out(s + 1, k, 1 - b)
                    for t in range(MT):
                        if task_end[t] + 3 == u:
                            key_high(s + 1, t)

            stages(act, stage)
            after_act(act, split_w, ln_hi)

        @block.vector
        def _(dve):
            step_no = [0]

            def step(ins):
                ins.then_inc(dve_step, 1)
                step_no[0] = step_no[0] + 1
                dve.wait_ge(dve_step, step_no[0])

            def rsqrt(v, cols, res):
                y, t = nt_y[:, 0:cols], nt_t[:, 0:cols]
                step(nc.vector.tensor_scalar(y.bitcast(I32), v.bitcast(I32), -0.5, RSQRT_MAGIC, ALU.mult, ALU.add))
                for k in range(NEWTON):
                    step(nc.vector.tensor_tensor(t, y, y, ALU.mult))
                    step(nc.vector.scalar_tensor_tensor(t, t, -0.5, v, ALU.mult, ALU.mult))
                    last = nc.vector.scalar_tensor_tensor(res if k == NEWTON - 1 else y, t, 1.5, y, ALU.add, ALU.mult)
                    if k < NEWTON - 1:
                        step(last)
                return last

            def split_w(j):
                src, hi, lo, slot = w_jobs[j]
                dve.wait_ge(w_hi_ready, j + 1)
                nc.vector.scalar_tensor_tensor(lo, slots[slot], W_SCALE, hi, ALU.mult, ALU.subtract).then_inc(w_split, 1)

            def ctx_lo(c, b):
                dve.wait_ge(ctx_hi_ready, c + 1)
                nc.vector.scalar_tensor_tensor(ctx_hl[b][1], ctx_f, ACT_SCALE, ctx_hl[b][0], ALU.mult,
                                               ALU.subtract).then_inc(ctx_split, 1)

            def ln_tile(t, ln, src, norm, front):
                for k in range(2):
                    step(nc.vector.bn_stats(bn[:, k, :], src[:, t, 512 * k:512 * k + 512]))
                step(nc.vector.bn_aggr(mv[:, t, :], bn[:, :, :]))
                step(nc.vector.tensor_scalar(nt_v[:, 0:1], mv[:, t, 1:2], 1e-5, None, ALU.add))
                step(rsqrt(nt_v[:, 0:1], 1, rs_ln[:, t:t + 1]))
                if t >= 2:
                    dve.wait_ge(front_ready, front + 2 * (t - 1))
                nc.vector.tensor_scalar(norm[t % 2], src[:, t], mv[:, t, 0:1], rs_ln[:, t:t + 1], ALU.subtract,
                                        ALU.mult).then_inc(normed, 1)

            def ln_lo(t, q, front, ln, hl):
                dve.wait_ge(ln_hi_ready, ln * 2 * TT + 2 * t + q + 1)
                at = (slice(None), slice(4 * q, 4 * q + 4), slice(t * P, (t + 1) * P))
                nc.vector.scalar_tensor_tensor(hl[1][at], ps[:, front % 4, :].rearrange("p (d n) -> p d n", n=P),
                                               ACT_SCALE, hl[0][at], ALU.mult, ALU.subtract).then_inc(front_free, 1)

            def layernorm(ln, src, norm, hl, front, tile_ready):
                for t in range(TT + 1):
                    if t < TT:
                        tile_ready(t)
                        ln_tile(t, ln, src, norm, front)
                    if t >= 1:
                        for q in range(2):
                            ln_lo(t - 1, q, front + 2 * (t - 1) + q, ln, hl)

            def key_stats(c, t):
                dve.wait_ge(key_sq_ready, c * MT + (t + 1))
                v = nt_v[:, 0:HP]
                step(nc.vector.reduce_sum(v, keys_sq[t], axis=AX_X))
                step(nc.vector.tensor_scalar(v, v, 1.0 / (DH1 * ACT_SCALE ** 2), 1e-6 / ACT_SCALE ** 2, ALU.mult, ALU.add))
                rsqrt(v, HP, rs_key[t][:, :]).then_inc(key_rs_ready, 1)

            layernorm(0, x_a, norm_a, xa_hl, FRONT_LN1, lambda t: dve.wait_ge(x_loaded[t], 16))
            for j in range(W_Q, W_KV):
                split_w(j)
            for t in range(TT):
                raw = q_raw[t % 2]
                dve.wait_ge(work_out, work_no["q", t, 1] + 1)
                step(nc.vector.tensor_tensor(q_sq, raw, raw, ALU.mult))
                step(nc.vector.reduce_sum(nt_v[:, :], q_sq, axis=AX_X))
                step(nc.vector.tensor_scalar(nt_v[:, :], nt_v[:, :], 1.0 / (DH1 * ACT_SCALE ** 2), 1e-6 / ACT_SCALE ** 2,
                                             ALU.mult, ALU.add))
                step(rsqrt(nt_v[:, :], H1, rs_q[:, :]))
                nc.vector.tensor_tensor(raw, raw, rs_q[:, :].unsqueeze(2).to_broadcast([P, H1, DH1]),
                                        ALU.mult).then_inc(q_normed, 1)
                for h in range(2):
                    split_w(W_KV + 2 * t + h)
                if t == 0:
                    ctx_lo(0, 0)
                if t == 2:
                    ctx_lo(1, 1)
                dve.wait_ge(q_hi, t + 1)
                nc.vector.tensor_tensor(q_stack[t % 2][:, :, 2:4, :], raw.unsqueeze(2).to_broadcast([P, H1, 2, DH1]),
                                        q_stack[t % 2][:, :, 0:2, :], ALU.subtract).then_inc(q_stacked, 1)
            for n in range(NT):
                if n in (1, 2):
                    key_stats(0, n - 1)
                split_w(W_KV2 + n)
            steps0 = step_no[0]
            STEPS = MT * (3 + 3 * NEWTON - 1)

            def add_outs(count, p, g, bank, first):
                at_least(dve, pv_done, (count + 1) * MT)
                at_least(dve, outs_added, count)
                if first:
                    ins = nc.vector.tensor_copy(att[:, p * GP + g], ps[:, bank, :])
                else:
                    ins = nc.vector.tensor_tensor(att[:, p * GP + g], ps[:, bank, :], att[:, p * GP + g], ALU.add)
                ins.then_inc(outs_added, 1)

            def stage(s, b, p):
                project = not (isinstance(s, int) and s + 1 >= STAGES)
                step_no[0] = s * STEPS + steps0
                first = first_of_pass(s)
                second = isinstance(s, int) and s % NCH == 1
                for u in range(UNITS):
                    g, t, head = unit(u)
                    n = s * UNITS + u
                    dve.wait_ge(probs_ready, n + 1)
                    at_least(dve, probs_summed, n - 1)
                    acc = prob_sum[:, head * N:(head + 2) * N]
                    if first and t == 0:
                        ins = nc.vector.tensor_copy(acc, probs[u % 4])
                    else:
                        ins = nc.vector.tensor_tensor(acc, acc, probs[u % 4], ALU.add)
                    ins.then_inc(probs_summed, 1)
                    if u % 4 == 1 and not (first and u == 1):
                        g = (u - 2) // 4 % GP
                        add_outs(s * GP + (u - 2) // 4, p, g, OUTS + g % 2, (first and u > 1) or (second and u == 1))
                    if isinstance(s, int) and s in (NCH, NCH + 1) and u in W_STEPS:
                        split_w(W_SA + (s - NCH) * 4 + W_STEPS.index(u))
                    if not project:
                        continue
                    if u == 2 and not (isinstance(s, int) and s + 2 >= STAGES):
                        ctx_lo(s + 2, b)
                    for t in range(MT):
                        if task_end[t] + 1 == u:
                            key_stats(s + 1, t)
                if last_of_pass(s):
                    add_outs(s * GP + GP - 1, p, GP - 1, OUTS + (GP - 1) % 2, False)
                    for g in range(GP):
                        front = FRONT_DEN + p * GP + g
                        dve.wait_ge(front_ready, front + 1)
                        nc.vector.reciprocal(rden, ps[:, front % 4, :]).then_inc(front_free, 1)
                        dve.wait_ge(front_free, front + 1)
                        at_least(dve, outs_added, (s + 1) * GP)
                        nc.vector.tensor_tensor(att[:, p * GP + g], att[:, p * GP + g], rden, ALU.mult)\
                            .then_inc(att_ready, 1)
                        dve.wait_ge(att_ready, p * GP + g + 1)

            stages(dve, stage)
            after_dve(dve, step, split_w, layernorm)

        @block.tensor
        def _(pe):
            def transpose_tokens(front0, norm, ln):
                for t in range(TT):
                    pe.wait_ge(normed, ln * TT + t + 1)
                    for q in range(2):
                        f = front0 + 2 * t + q
                        at_least(pe, front_free, f - 3)
                        for k in range(4):
                            d = 4 * q + k
                            last = nc.tensor.transpose(ps[:, f % 4, k * P:(k + 1) * P], norm[t % 2][:, d * P:(d + 1) * P],
                                                       ident[:, :])
                        last.then_inc(front_ready, 1)

            def split_product(dst, left, right, i, last_item):
                d, k = divmod(i, 3)
                a, b_ = ((0, 0), (0, 1), (1, 0))[k]
                return nc.tensor.matmul(dst, left[a](d), right[b_](d), start=(i == 0), stop=last_item)

            pe.wait_ge(ident_ready, 5)
            transpose_tokens(FRONT_LN1, norm_a, 0)
            pe.wait_ge(w_split, W_KV)
            pe.wait_ge(front_free, FRONT_LN1 + 2 * TT)
            for task in q_order:
                kind, t, h = task
                no = work_no[task]
                at_least(pe, work_out, no - 1)
                if kind == "q":
                    left = [lambda d, v=v: v[:, d, t * P:(t + 1) * P] for v in xa_hl]
                    right = [lambda d, v=v: v[:, d, 512 * h:512 * h + 512] for v in wq]
                    for i in range(3 * DC):
                        last = split_product(ps[:, WORK + no % 2, :], left, right, i, i == 3 * DC - 1)
                else:
                    if h == 0:
                        pe.wait_ge(q_stacked, t + 1)
                    for k in range(8):
                        last = nc.tensor.transpose(ps[:, WORK + no % 2, :].bitcast(F16)[:, k * P:(k + 1) * P],
                                                   q_stack[t % 2][:, 8 * h + k].rearrange("p s d -> p (s d)"), ident16[:, :])
                last.then_inc(work_ready, 1)

            def chunk_item(c, b, p, item):
                n, i, ends = item
                kind, t, h = TASKS[n]
                bank = ps[:, WORK + TASK_BANK[n], :]
                if i == 0:
                    pe.wait_ge(work_out, c * NT + (W0 + TASK_FREE[n]))
                    if n == 0:
                        pe.wait_ge(ctx_split, c + 1)
                    if kind == "T" and h == 0:
                        pe.wait_ge(key_stacked, c * MT + (t + 1))
                if kind == "T":
                    ins = nc.tensor.transpose(bank.bitcast(F16)[:, i * P:(i + 1) * P],
                                              key_stack[t][:, 8 * h + i].rearrange("p s d -> p (s d)"), ident16[:, :])
                else:
                    w0 = 0 if kind == "K" else KW
                    left = [lambda d, v=v: v[:, d, t * P:(t + 1) * P] for v in ctx_hl[b]]
                    right = [lambda d, v=v: v[:, d, w0:w0 + KW] for v in wkv[p]]
                    ins = split_product(bank, left, right, i, ends)
                if ends:
                    ins.then_inc(work_ready, 1)

            def times_values(q, b, p, count):
                g, t, head = unit(2 * q)
                if t == 0:
                    at_least(pe, outs_added, count - 1)
                for j in range(4):
                    last = nc.tensor.matmul(ps[32 * j:32 * j + 32, OUTS + g % 2, :],
                                            values[b][:, t, (head + j) * DH1:(head + j + 1) * DH1],
                                            probs[(2 * q + j // 2) % 4][:, j % 2 * N:(j % 2 + 1) * N],
                                            start=(t == 0), stop=(t == MT - 1))
                last.then_inc(pv_done, 1)

            pe.wait_ge(w_split, W_KV2)
            for its in per_step:
                for it in its:
                    chunk_item(0, 0, 0, it)

            def stage(s, b, p):
                project = not (isinstance(s, int) and s + 1 >= STAGES)
                for u in range(UNITS):
                    g, t, head = unit(u)
                    n = s * UNITS + u
                    if u == 0:
                        pe.wait_ge(work_out, s * NT + (W0 + 4))
                        if first_of_pass(s):
                            at_least(pe, front_free, FRONT_DEN + p * GP)
                    if u == 2:
                        pe.wait_ge(work_out, s * NT + (W0 + 7))
                    if u == 5:
                        pe.wait_ge(work_out, s * NT + (W0 + 8))
                    at_least(pe, probs_ready, n - 1)
                    for k in range(2):
                        last = nc.tensor.matmul(ps[:, SCORES + 2 * (u % 2) + k, :],
                                                kT[b][:, head + k, t * P:(t + 1) * P], qT[p][:, head + k, :],
                                                start=True, stop=True)
                    last.then_inc(scores_ready, 1)
                    if u % 2 and u >= 3:
                        times_values((u - 3) // 2, b, p, s * GP + (u - 3) // 4)
                    elif u == 1 and not first_of_pass(s):
                        times_values(UNITS // 2 - 1, 1 - b, p, s * GP - 1)
                    if project:
                        if u == 0 and last_of_pass(s):
                            pe.wait_ge(w_split, W_END)
                        for it in per_step[u]:
                            chunk_item(s + 1, 1 - b, pass_of_next(s, p), it)
                if last_of_pass(s):
                    pe.wait_ge(probs_ready, (s + 1) * UNITS)
                    times_values(UNITS // 2 - 1, b, p, s * GP + GP - 1)
                    pe.wait_ge(probs_summed, (s + 1) * UNITS)
                    for g in range(GP):
                        f = FRONT_DEN + p * GP + g
                        for j in range(4):
                            head = 4 * g + j
                            last = nc.tensor.matmul(ps[32 * j:32 * j + 32, f % 4, :], ones[:, :],
                                                    prob_sum[:, head * N:(head + 1) * N], start=True, stop=True)
                        last.then_inc(front_ready, 1)

            stages(pe, stage)
            after_pe(pe, transpose_tokens, split_product)


def laid_out(inputs):
    import numpy as np

    def tiles(w, cols):
        d, c = w.shape
        return w.reshape(d // 128, 128, c // cols, cols).transpose(2, 1, 0, 3)

    a = {k: np.asarray(v) for k, v in inputs.items()}
    wkv = np.concatenate([a["L0_xattn_Wk"], a["L0_xattn_Wv"]], 0)
    wkv = wkv.reshape(2, 512, 2, wkv.shape[1]).transpose(3, 0, 2, 1)
    return {
        "x": a["x"][0],
        "ctx_t": tiles(a["ctx_2048"][0].T, 256),
        "wq_t": a["L0_xattn_Wq"].T,
        "wkv_t": wkv.reshape(wkv.shape[0], -1),
        "wqkv_t": a["L0_attn_Wqkv"].T,
        "wproj_t": a["L0_attn_Wproj"].T,
        "wg_t": tiles(a["L0_ffn_wq_gate"].T, 128),
        "wu_t": tiles(a["L0_ffn_wq_up"].T, 128),
        "wd_t": a["L0_ffn_wq_down"].T,
        "s_gate": a["L0_ffn_s_gate"].reshape(-1, 128).T,
        "s_up": a["L0_ffn_s_up"].reshape(-1, 128).T,
        "s_down": a["L0_ffn_s_down"].reshape(1, -1),
    }


def kernel(**inputs):
    import numpy as np
    import concourse.bacc as bacc
    from concourse import mybir as mb
    from concourse.bass_utils import run_bass_kernel_spmd

    nc = bacc.Bacc("TRN2", target_bir_lowering=False, num_devices=1, dynamic_dma_scratch_size=1024)
    arrays, args = {}, []
    for name, a in laid_out(inputs).items():
        a = np.ascontiguousarray(a)
        arrays["in_" + name] = a
        args.append(nc.dram_tensor("in_" + name, a.shape, mb.dt.from_np(a.dtype), kind="ExternalInput").ap())
    shape = tuple(np.asarray(inputs["x"]).shape)
    args.append(nc.dram_tensor("out_0", shape[1:], mb.dt.float32, kind="ExternalOutput").ap())
    build_perceiver(nc, *args)
    r = run_bass_kernel_spmd(nc, [arrays], core_ids=[0])
    return np.asarray(r.results[0]["out_0"]).reshape(shape)
```

```python
from contextlib import ExitStack

import concourse.bass as bass
from concourse import mybir

F32 = mybir.dt.float32
F16 = mybir.dt.float16
I32 = mybir.dt.int32
ALU = mybir.AluOpType
ACT = mybir.ActivationFunctionType
AX_X = mybir.AxisListType.X

P = 128
ACT_SCALE = 64.0
W_SCALE = 1024.0
HID_SCALE = 16.0
PROD = ACT_SCALE * W_SCALE
RSQRT_MAGIC = 1597463007.0
NEWTON = 3


def build_perceiver(nc, x, ctx_t, wq_t, wkv_t, wqkv_t, wproj_t, wg_t, wu_t, wd_t, s_gate, s_up, s_down, out):
    N, D = x.shape
    CM = ctx_t.shape[3]
    M = ctx_t.shape[0] * CM
    HID = wd_t.shape[0]
    H1, DH1 = 32, D // 32
    H2, DH2 = 16, D // 16
    TT = N // P
    DC = D // P
    MT = CM // P
    NCH = M // CM
    PASSES = 2
    HP = H1 // PASSES
    GP = HP // 4
    UNITS = GP * MT * 2
    STAGES = PASSES * NCH
    HT = HID // P
    KW = HP * DH1
    assert N == 512 and D == 1024 and KW == 512 and M % CM == 0 and HID % P == 0

    with ExitStack() as stack:
        def sb(name, shape, dt):
            return stack.enter_context(nc.sbuf_tensor(name, shape, dt))

        def sem(name):
            return stack.enter_context(nc.semaphore(name))

        KB = 256
        arena = sb("arena", [P, 220 * KB], F32)

        def region(at_kb, kb, dt=F32):
            r = arena[:, int(at_kb * KB):int((at_kb + kb) * KB)]
            return r if dt == F32 else r.bitcast(dt)

        def pair(at_kb, kb, cols):
            v = region(at_kb, kb, F16).rearrange("p (s d c) -> p s d c", s=2, c=cols)
            return v[:, 0], v[:, 1]

        wkv = [pair(32 * p, 32, 2 * KW) for p in range(PASSES)]
        qT = [region(64 + 16 * p, 16, F16).rearrange("p (h n) -> p h n", n=N) for p in range(PASSES)]
        kT = [region(96 + 8 * b, 8, F16).rearrange("p (h m) -> p h m", m=CM) for b in range(2)]
        values = [region(112 + 4 * b, 4).rearrange("p (t c) -> p t c", c=KW) for b in range(2)]
        ctx_f = region(120, 8).rearrange("p (d m) -> p d m", m=CM)
        ctx_hl = [pair(128 + 8 * b, 8, CM) for b in range(2)]
        keys = [region(144 + 2 * t, 2).rearrange("p (h d) -> p h d", d=DH1) for t in range(MT)]
        key_stack = [region(148 + 4 * t, 4, F16).rearrange("p (h s d) -> p h s d", s=4, d=DH1) for t in range(MT)]
        keys_sq = [region(148 + 4 * t, 2).rearrange("p (h d) -> p h d", d=DH1) for t in range(MT)]
        probs = [region(156 + 4 * b, 4) for b in range(4)]
        prob_sum = region(172, 32)
        att = region(204, 16).rearrange("p (g n) -> p g n", n=N)
        x_a = region(166, 16).rearrange("p (t c) -> p t c", c=D)
        xa_hl = pair(182, 16, N)
        norm_a = [region(198 + 4 * b, 4) for b in range(2)]
        q_raw = [region(206 + 4 * b, 4).rearrange("p (h d) -> p h d", d=DH1) for b in range(2)]
        q_sq = region(150, 4).rearrange("p (h d) -> p h d", d=DH1)
        q_stack = [region(96 + 8 * b, 8, F16).rearrange("p (h s d) -> p h s d", s=4, d=DH1) for b in range(2)]
        wq = pair(32, 32, D)
        x1 = region(64, 16).rearrange("p (t c) -> p t c", c=D)
        wqkv = [pair(at_, 32, D) for at_ in (0, 32, 166)]
        wproj = pair(0, 32, D)
        xb_hl = pair(80, 16, N)
        norm_b = [region(128 + 4 * b, 4) for b in range(2)]
        q2T = region(96, 16).rearrange("p (c n) -> p c n", n=N)
        k2T = region(144, 16).rearrange("p (c n) -> p c n", n=N)
        v2 = region(198, 16).rearrange("p (t c) -> p t c", c=D)
        sa_p = [region(136 + 2 * b, 2) for b in range(4)]
        sa_pT = [region(32 + 8 * b, 8).rearrange("p (k n) -> p k n", n=N) for b in range(2)]
        sa_out = pair(48, 16, N)
        mask = region(164, 2)
        sa_max, sa_neg, sa_sum, sa_inv = [region(160 + 0.25 * k, 0.25) for k in range(4)]
        w_stage = [region(112 + 4 * b, 4) for b in range(4)]
        ring = [[pair(166 + 8 * r + 4 * m, 4, P) for m in range(2)] for r in range(4)]
        w_down = [pair(4 * j if j < 16 else 140 + 4 * (j - 16), 4, D) for j in range(HT)]
        hid_at = [96 + 2 * j for j in range(8)] + [128 + 2 * j for j in range(6)] + [198 + 2 * j for j in range(8)]
        hid = [pair(a, 2, N) for a in hid_at]
        s_down_b = region(214, 4)
        silu_b = [region(164, 2), region(218, 2)]
        sg = sb("sg", [P, HT], F32)
        su = sb("su", [P, HT], F32)
        slots = [region(a, 4) for a in (214, 158, 162, 116, 120, 124, 64, 68, 0, 4, 8, 12, 16, 20, 24, 28)]

        ident = sb("ident", [P, P], F32)
        ident16 = sb("ident16", [P, P], F16)
        ones = sb("ones", [P, DH1], F32)
        bn = sb("bn", [P, 2, 6], F32)
        mv = sb("mv", [P, TT, 2], F32)
        nt_v = sb("nt_v", [P, 32], F32)
        nt_y = sb("nt_y", [P, 32], F32)
        nt_t = sb("nt_t", [P, 32], F32)
        rs_key = [sb(f"rs_key{t}", [P, HP], F32) for t in range(MT)]
        rs_q = sb("rs_q", [P, H1], F32)
        rs_ln = sb("rs_ln", [P, TT], F32)

        ps = stack.enter_context(nc.psum_tensor("ps", [P, 8, 512], F32))
        SCORES, OUTS, WORK = 0, 4, 6

        ident_ready = sem("ident_ready")
        x_loaded = [sem(f"x_loaded{t}") for t in range(TT)]
        ctx_loaded = sem("ctx_loaded")
        ctx_hi_ready = sem("ctx_hi_ready")
        ctx_split = sem("ctx_split")
        w_loaded = [sem(f"w_loaded{s}") for s in range(len(slots))]
        w_hi_ready = sem("w_hi_ready")
        w_split = sem("w_split")
        dve_step = sem("dve_step")
        normed = sem("normed")
        front_ready = sem("front_ready")
        ln_hi_ready = sem("ln_hi_ready")
        front_free = sem("front_free")
        work_ready = sem("work_ready")
        work_out = sem("work_out")
        q_sq_ready = sem("q_sq_ready")
        q_rs_ready = sem("q_rs_ready")
        q_normed = sem("q_normed")
        q_hi = sem("q_hi")
        q_stacked = sem("q_stacked")
        key_sq_ready = sem("key_sq_ready")
        key_rs_ready = sem("key_rs_ready")
        key_normed = sem("key_normed")
        key_hi = sem("key_hi")
        key_stacked = sem("key_stacked")
        scores_ready = sem("scores_ready")
        probs_ready = sem("probs_ready")
        probs_summed = sem("probs_summed")
        pv_done = sem("pv_done")
        outs_added = sem("outs_added")
        den_ready = sem("den_ready")
        den_out = sem("den_out")
        den_inverted = sem("den_inverted")
        att_ready = sem("att_ready")

        x_again = sem("x_again")
        sa_scores = sem("sa_scores")
        sa_masked = sem("sa_masked")
        sa_exp = sem("sa_exp")
        sa_norm = sem("sa_norm")
        sa_turned = sem("sa_turned")
        sa_turned_out = sem("sa_turned_out")
        sa_pv = sem("sa_pv")
        sa_out_hi = sem("sa_out_hi")
        sa_out_split = sem("sa_out_split")
        mask_ready = sem("mask_ready")
        proj_ready = sem("proj_ready")
        proj_added = sem("proj_added")
        f_loaded = [sem(f"f_loaded{b}") for b in range(4)]
        scales_loaded = sem("scales_loaded")
        scales_ready = sem("scales_ready")
        f_value = sem("f_value")
        f_hi = sem("f_hi")
        f_split = sem("f_split")
        gu_ready = sem("gu_ready")
        silu_ready = sem("silu_ready")
        hid_ready = sem("hid_ready")
        hid_hi = sem("hid_hi")
        hid_split = sem("hid_split")
        down_ready = sem("down_ready")
        down_scaled = sem("down_scaled")
        down_out = sem("down_out")
        stored = sem("stored")

        early = []
        for t in range(TT):
            early.append(("q", t, 0))
            if t >= 2:
                early += [("qt", t - 2, b) for b in range(H1 // 8)]
            early.append(("q", t, 1))
        for t in range(MT):
            early.append(("key", t, 0))
            early += [("qt", TT - 2 + t, b) for b in range(H1 // 8)]
        work_no = {task: n for n, task in enumerate(early)}
        W0 = len(early) - MT

        def key_no(c, t):
            return work_no["key", t, 0] if isinstance(c, int) and c == 0 else c * NT + (W0 + t)

        TASKS = [("K", 0, 0), ("K", 1, 0), ("T", 0, 0), ("T", 0, 1), ("V", 0, 0), ("T", 1, 0), ("T", 1, 1), ("V", 1, 0)]
        TASK_BANK = [0, 1, 1, 1, 0, 0, 0, 1]
        TASK_FREE = [-1, 0, 2, 3, 1, 5, 6, 4]
        NT = len(TASKS)
        products = [(TASKS.index((kind, t, 0)), i, i == 3 * DC - 1) for kind in "KV" for t in range(MT) for i in range(3 * DC)]
        PER_STEP = len(products) // UNITS
        T_STEPS = {9: ("T", 0, 0), 10: ("T", 0, 1), 13: ("T", 1, 0), 14: ("T", 1, 1)}
        per_step = [products[u * PER_STEP:(u + 1) * PER_STEP] +
                    [(TASKS.index(T_STEPS[u]), i, i == 7) for i in range(8) if u in T_STEPS] for u in range(UNITS)]
        task_end = {it[0]: u for u, its in enumerate(per_step) for it in its if it[2]}
        assert sorted(task_end, key=task_end.get) == list(range(NT))

        FRONT_LN1 = 0
        FRONT_BACK = FRONT_LN1 + 2 * TT
        FRONT_LN2 = FRONT_BACK + 2 * TT
        FRONT_LN3 = FRONT_LN2 + 2 * TT

        w_jobs = []
        for d in range(DC):
            w_jobs.append((wq_t[d * P:(d + 1) * P, :], wq[0][:, d], wq[1][:, d], 8 + d))
        for p in range(PASSES):
            for d in range(DC):
                w_jobs.append((wkv_t[d * P:(d + 1) * P, p * 1024:(p + 1) * 1024], wkv[p][0][:, d], wkv[p][1][:, d],
                               len(w_jobs) % 4))
        W_Q, W_KV, W_KV2, W_END = 0, DC, 2 * DC, 3 * DC
        W_SA = W_END
        SA_PARTS = (2, 0, 1)
        for k, part in enumerate(SA_PARTS):
            for d in range(DC):
                w_jobs.append((wqkv_t[d * P:(d + 1) * P, part * D:(part + 1) * D], wqkv[k][0][:, d],
                               wqkv[k][1][:, d], 6 + d % 2 if k == 0 else (4, 5, 0)[(len(w_jobs) - W_SA - DC) % 3]))
        W_PROJ = len(w_jobs)
        for d in range(DC):
            w_jobs.append((wproj_t[d * P:(d + 1) * P, :], wproj[0][:, d], wproj[1][:, d], (4, 5, 0)[(len(w_jobs) - W_SA - DC) % 3]))
        slot_use = []
        for j, job in enumerate(w_jobs):
            slot_use.append(sum(1 for k in w_jobs[:j] if k[3] == job[3]))
        slot_before = [max([k for k in range(j) if w_jobs[k][3] == w_jobs[j][3]], default=None) for j in range(len(w_jobs))]

        def unit(u):
            g, rest = divmod(u, 2 * MT)
            t, pr = divmod(rest, 2)
            return g, t, 4 * g + 2 * pr

        ctx_v = ctx_t.rearrange("c p d m -> c p (d m)")
        x_v = x.rearrange("(t p) c -> t p c", p=P)

        def at_least(eng, s, n):
            if not isinstance(n, int) or n > 0:
                eng.wait_ge(s, n)

        def stages(eng, emit):
            for p in range(PASSES):
                base = p * NCH
                emit(base, 0, p)
                emit(base + 1, 1, p)
                with eng.Fori(0, (NCH - 4) // 2) as i:
                    for b in range(2):
                        emit(i * 2 + (base + 2 + b), b, p)
                emit(base + NCH - 2, 0, p)
                emit(base + NCH - 1, 1, p)

        def last_of_pass(s):
            return isinstance(s, int) and s % NCH == NCH - 1

        def first_of_pass(s):
            return isinstance(s, int) and s % NCH == 0

        def denominators_due(s, u, p):
            if u % 4 == 0:
                if last_of_pass(s) and u >= 8:
                    return p, (u - 8) // 4
                if first_of_pass(s) and p and u < 4 * (GP - 2):
                    return p - 1, (u + 4 * GP - 8) // 4
            return None

        def group_den(g):
            return prob_sum[:, 4 * g * N:(4 * g + 1) * N]

        def pass_of_next(s, p):
            return p + 1 if last_of_pass(s) else p

        EARLY_SPLITS = (2, 3, 3, 4)
        W_STEPS = (4, 7, 10, 13)

        W1 = W0 + NT * STAGES
        SA_UNITS = H2 * TT
        SA_LAG = 3

        f_jobs = [(m, j) for j in range(4) for m in ("gate", "up")]
        for j in range(HT):
            f_jobs.append(("down", j))
            if j + 4 < HT:
                f_jobs += [("gate", j + 4), ("up", j + 4)]
        f_no = {job: n for n, job in enumerate(f_jobs)}
        F_AHEAD = 8
        CODE_SCALE = 2.0 ** -14
        GU_SCALE = 1.0 / (CODE_SCALE * ACT_SCALE)

        def f_dest(job):
            m, j = job
            if m == "down":
                return [v.rearrange("p a c -> p (a c)") for v in w_down[j]]
            return [v.rearrange("p a c -> p (a c)") for v in ring[j % 4][m == "up"]]

        def f_turn(j):
            return [f_no[job] for job in [("down", j), ("gate", j + 4), ("up", j + 4)] if job in f_no]

        def after_sp(sp, load_w):
            sp.wait_ge(ctx_split, STAGES)
            for j in range(W_SA + DC, len(w_jobs)):
                if j == W_SA + DC + 2:
                    sp.wait_ge(front_ready, FRONT_LN2)
                load_w(j)
            sp.dma_start(sg[:, :], s_gate).then_inc(scales_loaded, 16)
            sp.dma_start(su[:, :], s_up).then_inc(scales_loaded, 16)
            sp.wait_ge(w_split, len(w_jobs))
            sp.dma_start(s_down_b, s_down.to_broadcast([P, D])).then_inc(scales_loaded, 16)
            for n, (m, j) in enumerate(f_jobs):
                src = {"gate": lambda: wg_t[j].rearrange("p d c -> p (d c)"),
                       "up": lambda: wu_t[j].rearrange("p d c -> p (d c)"),
                       "down": lambda: wd_t[j * P:(j + 1) * P, :]}[m]()
                at_least(sp, f_split, n - 3)
                sp.dma_start(w_stage[n % 4].bitcast(I32), src).then_inc(f_loaded[n % 4], 16)
            for t in range(TT):
                for h in range(2):
                    sp.wait_ge(down_out, 2 * t + h + 1)
                    sp.dma_start(out[t * P:(t + 1) * P, 512 * h:512 * h + 512], x1[:, t, 512 * h:512 * h + 512])\
                        .then_inc(stored, 16)
            sp.wait_ge(stored, 16 * 2 * TT)

        def after_pool(pool):
            pool.wait_ge(att_ready, PASSES * GP)
            nc.gpsimd.memset(mask, 0.0).then_inc(mask_ready, 1)
            pool.wait_ge(mask_ready, 1)
            diagonal = mask[:, 3 * P:4 * P]
            nc.gpsimd.affine_select(out=diagonal, in_=diagonal, compare_op=ALU.is_ge, fill=-1e30, base=0,
                                    pattern=[[-1, P]], channel_multiplier=1).then_inc(mask_ready, 1)
            for j in range(HT):
                pool.wait_ge(hid_hi, j + 1)
                nc.gpsimd.tensor_tensor(hid[j][1][:, 0], silu_b[j % 2], hid[j][0][:, 0], ALU.subtract).then_inc(hid_split, 1)

        def after_act(act, split_w, ln_hi):
            for q in range(2):
                ln_hi(0, q, FRONT_LN2 + q, 1, xb_hl[0])
            for n in range(3 * DC):
                k, c = divmod(n, DC)
                act.wait_ge(work_ready, W1 + n + 1)
                dst = (v2[:, c // 2, 512 * (c % 2):512 * (c % 2) + 512], q2T[:, c], k2T[:, c])[k]
                nc.scalar.activation(dst, ps[:, WORK + n % 2, :], ACT.Copy, scale=1.0 / PROD).then_inc(work_out, 1)
                if n % 2 == 0 and n // 2 + 1 < TT:
                    for q in range(2):
                        ln_hi(n // 2 + 1, q, FRONT_LN2 + n + 2 + q, 1, xb_hl[0])
                if n < 2 * TT:
                    split_w(W_SA + DC + 2 * n)
                    split_w(W_SA + DC + 2 * n + 1)
                elif n >= 2 * DC:
                    split_w(W_PROJ + n - 2 * DC)
            for k in range(SA_UNITS + 9):
                if k < SA_UNITS:
                    L = (k % TT + 1) * P
                    act.wait_ge(sa_masked, k + 1)
                    at_least(act, sa_turned, k - 3)
                    nc.scalar.activation(sa_p[k % 4][:, 0:L], ps[:, k % 4, 0:L], ACT.Exp, bias=sa_neg[:, k:k + 1],
                                         scale=DH2 ** -0.5, accum_out=sa_sum[:, k:k + 1]).then_inc(sa_exp, 1)
                m = k - SA_LAG
                if 0 <= m < SA_UNITS:
                    h, t = divmod(m, TT)
                    act.wait_ge(sa_turned, m + 1)
                    at_least(act, sa_pv, h - 1)
                    nc.scalar.activation(sa_pT[h % 2][:, 0:t + 1, t * P:(t + 1) * P],
                                         ps[:, WORK + m % 2, 0:(t + 1) * P].rearrange("p (k n) -> p k n", n=P),
                                         ACT.Copy).then_inc(sa_turned_out, 1)
                if k >= 16 and k % 8 == 0 or k == SA_UNITS + 8:
                    i = k // 8 - 2
                    act.wait_ge(sa_pv, 2 * i + 2)
                    nc.scalar.activation(sa_out[0][:, i], ps[:, OUTS + i % 2, :], ACT.Copy,
                                         scale=ACT_SCALE).then_inc(sa_out_hi, 1)

            def f_high(n):
                act.wait_ge(f_value, n + 1)
                nc.scalar.activation(f_dest(f_jobs[n])[0], w_stage[n % 4], ACT.Copy).then_inc(f_hi, 1)

            for n in range(F_AHEAD):
                f_high(n)
                if n >= 2 and n % 2 == 0:
                    for q in range(2):
                        ln_hi(n // 2 - 1, q, FRONT_LN3 + n - 2 + q, 2, xb_hl[0])
            for q in range(2):
                ln_hi(TT - 1, q, FRONT_LN3 + 2 * (TT - 1) + q, 2, xb_hl[0])
            act.wait_ge(scales_ready, 1)
            for j in range(HT + 1):
                if j < HT:
                    act.wait_ge(gu_ready, 2 * j + 1)
                    at_least(act, hid_split, j - 1)
                    nc.scalar.activation(silu_b[j % 2], ps[:, (WORK, OUTS)[j % 2], :], ACT.Silu,
                                         scale=sg[:, j:j + 1]).then_inc(silu_ready, 1)
                if j >= 1:
                    act.wait_ge(hid_ready, j)
                    nc.scalar.activation(hid[j - 1][0][:, 0], silu_b[(j - 1) % 2], ACT.Copy).then_inc(hid_hi, 1)
                if j < HT:
                    act.wait_ge(gu_ready, 2 * j + 2)
                    for n in f_turn(j):
                        f_high(n)

        def after_dve(dve, step, split_w, ln_tile, ln_low):
            dve.wait_ge(x_again, 16)
            for k in range(2 * TT):
                q, t = divmod(k, TT)
                dve.wait_ge(front_ready, FRONT_BACK + k + 1)
                xs = x1[:, t, 512 * q:512 * q + 512]
                nc.vector.tensor_tensor(xs, ps[:, (FRONT_BACK + k) % 4, :], xs, ALU.add).then_inc(front_free, 1)
            dve.wait_ge(front_free, FRONT_BACK + 2 * TT)
            ln_tile(0, 1, x1, norm_b, FRONT_LN2)
            ln_low(0, 1, xb_hl, FRONT_LN2)
            ln_tile(1, 1, x1, norm_b, FRONT_LN2)
            for n in range(3 * DC):
                if n % 2 == 0 and n // 2 + 2 < TT:
                    ln_tile(n // 2 + 2, 1, x1, norm_b, FRONT_LN2)
                if n % 2 == 0 and n // 2 + 1 < TT:
                    ln_low(n // 2 + 1, 1, xb_hl, FRONT_LN2)
                if n < 2 * TT:
                    split_w(W_SA + DC + 2 * n)
                    split_w(W_SA + DC + 2 * n + 1)
                elif n >= 2 * DC:
                    split_w(W_PROJ + n - 2 * DC)
            dve.wait_ge(mask_ready, 2)
            for k in range(SA_UNITS + 9):
                if k < SA_UNITS:
                    L = (k % TT + 1) * P
                    s_ = ps[:, k % 4, 0:L]
                    dve.wait_ge(sa_scores, k + 1)
                    step(nc.vector.tensor_tensor_reduce(out=s_, in0=s_, in1=mask[:, 4 * P - L:4 * P], scale=1.0, scalar=-3e38,
                                                        op0=ALU.add, op1=ALU.max, accum_out=sa_max[:, k:k + 1]))
                    nc.vector.tensor_scalar(sa_neg[:, k:k + 1], sa_max[:, k:k + 1], -(DH2 ** -0.5), None, ALU.mult)\
                        .then_inc(sa_masked, 1)
                if 1 <= k <= SA_UNITS:
                    m = k - 1
                    L = (m % TT + 1) * P
                    dve.wait_ge(sa_exp, m + 1)
                    step(nc.vector.reciprocal(sa_inv[:, m:m + 1], sa_sum[:, m:m + 1]))
                    nc.vector.tensor_scalar(sa_p[m % 4][:, 0:L], sa_p[m % 4][:, 0:L], sa_inv[:, m:m + 1], None,
                                            ALU.mult).then_inc(sa_norm, 1)
                if k >= 16 and k % 8 == 0 or k == SA_UNITS + 8:
                    i = k // 8 - 2
                    dve.wait_ge(sa_out_hi, i + 1)
                    nc.vector.scalar_tensor_tensor(sa_out[1][:, i], ps[:, OUTS + i % 2, :], ACT_SCALE, sa_out[0][:, i],
                                                   ALU.mult, ALU.subtract).then_inc(sa_out_split, 1)

            def f_float(n):
                dve.wait_ge(f_loaded[n % 4], 16 * (n // 4 + 1))
                nc.vector.tensor_scalar(w_stage[n % 4], w_stage[n % 4].bitcast(I32), -128.0, CODE_SCALE, ALU.add,
                                        ALU.mult).then_inc(f_value, 1)

            def f_low(n):
                hi, lo = f_dest(f_jobs[n])
                dve.wait_ge(f_hi, n + 1)
                nc.vector.tensor_tensor(lo, w_stage[n % 4], hi, ALU.subtract).then_inc(f_split, 1)

            dve.wait_ge(scales_loaded, 48)
            step(nc.vector.tensor_scalar(su[:, :], su[:, :], GU_SCALE * HID_SCALE, None, ALU.mult))
            step(nc.vector.tensor_scalar(s_down_b, s_down_b, 1.0 / (CODE_SCALE * HID_SCALE), None, ALU.mult))
            nc.vector.tensor_scalar(sg[:, :], sg[:, :], GU_SCALE, None, ALU.mult).then_inc(scales_ready, 1)
            for k in range(2 * TT):
                t, h = divmod(k, 2)
                dve.wait_ge(proj_ready, k + 1)
                xs = x1[:, t, 512 * h:512 * h + 512]
                nc.vector.scalar_tensor_tensor(xs, ps[:, WORK + k % 2, :], 1.0 / PROD, xs, ALU.mult,
                                               ALU.add).then_inc(proj_added, 1)
                if h == 1:
                    dve.wait_ge(proj_added, k + 1)
                    ln_tile(t, 2, x1, norm_b, FRONT_LN3)
                f_float(k)
                if k >= 1:
                    f_low(k - 1)
                if t >= 1 and h == 0:
                    ln_low(t - 1, 2, xb_hl, FRONT_LN3)
            ln_low(TT - 1, 2, xb_hl, FRONT_LN3)
            f_low(F_AHEAD - 1)
            for j in range(HT):
                turn = f_turn(j)
                f_float(turn[0])
                dve.wait_ge(silu_ready, j + 1)
                dve.wait_ge(gu_ready, 2 * j + 2)
                nc.vector.scalar_tensor_tensor(silu_b[j % 2], ps[:, (WORK, OUTS)[j % 2] + 1, :], su[:, j:j + 1],
                                               silu_b[j % 2], ALU.mult, ALU.mult).then_inc(hid_ready, 1)
                for n in turn[1:]:
                    f_float(n)
                    f_low(n - 1)
                f_low(turn[-1])
            for k in range(2 * TT):
                t, h = divmod(k, 2)
                b = ps[:, k % 4, :]
                xs = x1[:, t, 512 * h:512 * h + 512]
                dve.wait_ge(down_ready, k + 1)
                nc.vector.tensor_tensor(b, b, s_down_b[:, 512 * h:512 * h + 512], ALU.mult).then_inc(down_scaled, 1)
                dve.wait_ge(down_scaled, k + 1)
                nc.vector.tensor_tensor(xs, b, xs, ALU.add).then_inc(down_out, 1)

        def after_pe(pe, transpose_tokens, split_product):
            for k in range(2 * TT):
                q, t = divmod(k, TT)
                f = FRONT_BACK + k
                if t == 0:
                    pe.wait_ge(att_ready, (q + 1) * GP)
                pe.wait_ge(front_free, f - 3)
                for g in range(4):
                    last = nc.tensor.transpose(ps[:, f % 4, g * P:(g + 1) * P], att[:, 4 * q + g, t * P:(t + 1) * P],
                                               ident[:, :])
                last.then_inc(front_ready, 1)
            transpose_tokens(0, FRONT_LN2, norm_b, 1)
            for n in range(3 * DC):
                k, c = divmod(n, DC)
                pe.wait_ge(work_out, W1 + n - 1)
                if c == 0:
                    pe.wait_ge(w_split, W_SA + (k + 1) * DC)
                if k:
                    left = [lambda d, v=v: v[:, d, c * P:(c + 1) * P] for v in wqkv[k]]
                    right = [lambda d, v=v: v[:, d, :] for v in xb_hl]
                else:
                    t, h = divmod(c, 2)
                    if h == 0:
                        pe.wait_ge(front_free, FRONT_LN2 + 2 * (t + 1))
                    left = [lambda d, v=v: v[:, d, t * P:(t + 1) * P] for v in xb_hl]
                    right = [lambda d, v=v: v[:, d, 512 * h:512 * h + 512] for v in wqkv[0]]
                for i in range(3 * DC):
                    last = split_product(ps[:, WORK + n % 2, :], left, right, i, i == 3 * DC - 1)
                last.then_inc(work_ready, 1)
                if k == 0 and h == 0 and t + 1 < TT:
                    transpose_tokens(t + 1, FRONT_LN2, norm_b, 1)

            pe.wait_ge(work_out, W1 + 3 * DC)
            for k in range(SA_UNITS + SA_LAG + 3):
                if k < SA_UNITS:
                    h, t = divmod(k, TT)
                    at_least(pe, sa_exp, k - 3)
                    rows = slice(64 * (h % 2), 64 * (h % 2) + 64)
                    nc.tensor.matmul(ps[:, k % 4, 0:(t + 1) * P], q2T[rows, h // 2, t * P:(t + 1) * P],
                                     k2T[rows, h // 2, 0:(t + 1) * P], start=True, stop=True).then_inc(sa_scores, 1)
                m = k - SA_LAG
                if 0 <= m < SA_UNITS:
                    t = m % TT
                    pe.wait_ge(sa_norm, m + 1)
                    at_least(pe, sa_turned_out, m - 1)
                    for c in range(t + 1):
                        last = nc.tensor.transpose(ps[:, WORK + m % 2, c * P:(c + 1) * P], sa_p[m % 4][:, c * P:(c + 1) * P],
                                                   ident[:, :])
                    last.then_inc(sa_turned, 1)
                m -= 2
                if m >= 0 and m % TT == TT - 1:
                    h = m // TT
                    pe.wait_ge(sa_turned_out, m + 1)
                    if h % 2 == 0:
                        at_least(pe, sa_out_split, h // 2 - 1)
                    for c in range(TT):
                        last = nc.tensor.matmul(ps[64 * (h % 2):64 * (h % 2) + 64, OUTS + h // 2 % 2, c * P:N],
                                                v2[:, c, h * DH2:(h + 1) * DH2], sa_pT[h % 2][:, c, c * P:N],
                                                start=(c == 0), stop=(c == TT - 1))
                    last.then_inc(sa_pv, 1)

            pe.wait_ge(w_split, len(w_jobs))
            pe.wait_ge(sa_out_split, H2 // 2)
            for k in range(2 * TT):
                t, h = divmod(k, 2)
                at_least(pe, proj_added, k - 1)
                left = [lambda d, v=v: v[:, d, t * P:(t + 1) * P] for v in sa_out]
                right = [lambda d, v=v: v[:, d, 512 * h:512 * h + 512] for v in wproj]
                for i in range(3 * DC):
                    last = split_product(ps[:, WORK + k % 2, :], left, right, i, i == 3 * DC - 1)
                last.then_inc(proj_ready, 1)
                if t >= 1 and h == 0:
                    transpose_tokens(t - 1, FRONT_LN3, norm_b, 2)
            transpose_tokens(TT - 1, FRONT_LN3, norm_b, 2)
            pe.wait_ge(front_free, FRONT_LN3 + 2 * TT)
            for j in range(HT):
                pe.wait_ge(f_split, f_no["up", j] + 1)
                for m in range(2):
                    at_least(pe, (silu_ready, hid_ready)[m], j - 1)
                    left = [lambda d, v=v: v[:, d, :] for v in ring[j % 4][m]]
                    right = [lambda d, v=v: v[:, d, :] for v in xb_hl]
                    for i in range(3 * DC):
                        last = split_product(ps[:, (WORK, OUTS)[j % 2] + m, :], left, right, i, i == 3 * DC - 1)
                    last.then_inc(gu_ready, 1)
            pe.wait_ge(hid_split, HT)
            pe.wait_ge(f_split, len(f_jobs))
            for k in range(2 * TT):
                t, h = divmod(k, 2)
                at_least(pe, down_out, k - 3)
                left = [lambda j, v=v: hid[j][v][:, 0, t * P:(t + 1) * P] for v in range(2)]
                right = [lambda j, v=v: w_down[j][v][:, 0, 512 * h:512 * h + 512] for v in range(2)]
                for i in range(3 * HT):
                    last = split_product(ps[:, k % 4, :], left, right, i, i == 3 * HT - 1)
                last.then_inc(down_ready, 1)

        block = stack.enter_context(nc.Block())

        @block.sync
        def _(sp):
            for t in range(TT):
                sp.dma_start(x_a[:, t], x_v[t]).then_inc(x_loaded[t], 16)

            def load_w(j):
                src, _, _, slot = w_jobs[j]
                if slot_before[j] is not None:
                    sp.wait_ge(w_split, slot_before[j] + 1)
                sp.dma_start(slots[slot], src).then_inc(w_loaded[slot], 16)

            def load_ctx(c, chunk):
                at_least(sp, ctx_split, c)
                sp.dma_start(region(120, 8), ctx_v[bass.ds(chunk, 1)].rearrange("c p x -> (c p) x"))\
                    .then_inc(ctx_loaded, 16)

            for j in range(W_KV):
                load_w(j)
            load_ctx(0, 0)
            for j in range(W_KV, W_KV2):
                load_w(j)
            load_ctx(1, 1)
            for j in range(W_KV2, W_END):
                load_w(j)
            load_ctx(2, 2)
            with sp.Fori(0, NCH - 3) as i:
                load_ctx(i + 3, i + 3)
            for k in range(3):
                load_ctx(NCH + k, k)
            sp.wait_ge(scores_ready, NCH * UNITS)
            load_w(W_END)
            load_w(W_END + 1)
            load_ctx(NCH + 3, 3)
            for j in range(W_END + 2, W_SA + DC):
                load_w(j)
            sp.wait_ge(w_split, W_SA + DC)
            sp.dma_start(x1, x.rearrange("(t p) c -> p t c", p=P)).then_inc(x_again, 16)
            with sp.Fori(0, NCH - 4) as i:
                load_ctx(i + (NCH + 4), i + 4)
            after_sp(sp, load_w)

        @block.gpsimd
        def _(pool):
            nc.gpsimd.memset(ident[:, :], 0.0).then_inc(ident_ready, 1)
            nc.gpsimd.memset(ident16[:, :], 0.0).then_inc(ident_ready, 1)
            nc.gpsimd.memset(ones[:, :], 1.0).then_inc(ident_ready, 1)
            pool.wait_ge(ident_ready, 3)
            for m in (ident, ident16):
                nc.gpsimd.affine_select(out=m[:, :], in_=m[:, :], compare_op=ALU.not_equal, fill=1.0, base=0,
                                        pattern=[[-1, P]], channel_multiplier=1).then_inc(ident_ready, 1)

            def key_tile(c, t):
                n = c * MT + t
                pool.wait_ge(work_out, key_no(c, t) + 1)
                nc.gpsimd.tensor_tensor(keys_sq[t], keys[t], keys[t], ALU.mult).then_inc(key_sq_ready, 1)
                pool.wait_ge(key_rs_ready, n + 1)
                nc.gpsimd.tensor_tensor(keys[t], keys[t], rs_key[t][:, :].unsqueeze(2).to_broadcast([P, HP, DH1]),
                                        ALU.mult).then_inc(key_normed, 1)
                pool.wait_ge(key_hi, n + 1)
                nc.gpsimd.tensor_tensor(key_stack[t][:, :, 1::2, :],
                                        keys[t].unsqueeze(2).to_broadcast([P, HP, 2, DH1]),
                                        key_stack[t][:, :, 0::2, :], ALU.subtract).then_inc(key_stacked, 1)

            def stage(s, b, p):
                if not (isinstance(s, int) and s + 1 >= STAGES):
                    for t in range(MT):
                        key_tile(s + 1, t)

            for t in range(TT):
                raw = q_raw[t % 2]
                pool.wait_ge(work_out, work_no["q", t, 1] + 1)
                nc.gpsimd.tensor_tensor(q_sq, raw, raw, ALU.mult).then_inc(q_sq_ready, 1)
                pool.wait_ge(q_rs_ready, t + 1)
                nc.gpsimd.tensor_tensor(raw, raw, rs_q[:, :].unsqueeze(2).to_broadcast([P, H1, DH1]),
                                        ALU.mult).then_inc(q_normed, 1)
            for t in range(MT):
                key_tile(0, t)
            stages(pool, stage)
            after_pool(pool)

        @block.scalar
        def _(act):
            def split_w(j):
                src, hi, _, slot = w_jobs[j]
                act.wait_ge(w_loaded[slot], 16 * (slot_use[j] + 1))
                nc.scalar.activation(hi, slots[slot], ACT.Copy, scale=W_SCALE).then_inc(w_hi_ready, 1)

            def ln_hi(t, q, front, ln, hi):
                act.wait_ge(front_ready, front + 1)
                nc.scalar.activation(hi[:, 4 * q:4 * q + 4, t * P:(t + 1) * P],
                                     ps[:, front % 4, :].rearrange("p (d n) -> p d n", n=P), ACT.Copy,
                                     scale=ACT_SCALE).then_inc(ln_hi_ready, 1)

            def ctx_hi(c, b):
                act.wait_ge(ctx_loaded, (c + 1) * 16)
                nc.scalar.activation(ctx_hl[b][0], ctx_f, ACT.Copy, scale=ACT_SCALE).then_inc(ctx_hi_ready, 1)

            def copy_out(c, n, b):
                kind, t, h = TASKS[n]
                no = key_no(c, t) if kind == "K" else c * NT + (W0 + n)
                bank = WORK + TASK_BANK[n]
                act.wait_ge(work_ready, no + 1)
                if kind == "K":
                    at_least(act, key_stacked, c * MT + (t - 1))
                    nc.scalar.activation(keys[t], ps[:, bank, :].rearrange("p (h d) -> p h d", d=DH1), ACT.Copy,
                                         scale=1.0 / PROD).then_inc(work_out, 1)
                elif kind == "V":
                    nc.scalar.activation(values[b][:, t], ps[:, bank, :], ACT.Copy,
                                         scale=1.0 / PROD).then_inc(work_out, 1)
                else:
                    nc.scalar.activation(kT[b][:, 8 * h:8 * h + 8, t * P:(t + 1) * P],
                                         ps[:, bank, :].bitcast(F16).rearrange("p (h m) -> p h m", m=P),
                                         ACT.Copy).then_inc(work_out, 1)

            def key_high(c, t):
                act.wait_ge(key_normed, c * MT + (t + 1))
                nc.scalar.activation(key_stack[t][:, :, 0::2, :], keys[t].unsqueeze(2).to_broadcast([P, HP, 2, DH1]),
                                     ACT.Copy).then_inc(key_hi, 1)

            def q_high(t):
                act.wait_ge(q_normed, t + 1)
                nc.scalar.activation(q_stack[t % 2][:, :, 0:2, :], q_raw[t % 2].unsqueeze(2).to_broadcast([P, H1, 2, DH1]),
                                     ACT.Copy).then_inc(q_hi, 1)

            def early_out(task):
                kind, t, h = task
                no = work_no[task]
                act.wait_ge(work_ready, no + 1)
                bank = ps[:, WORK + no % 2, :]
                if kind == "q":
                    if t >= 2 and h == 0:
                        act.wait_ge(q_stacked, t - 1)
                    nc.scalar.activation(q_raw[t % 2][:, 16 * h:16 * h + 16], bank.rearrange("p (h d) -> p h d", d=DH1),
                                         ACT.Copy, scale=1.0 / PROD).then_inc(work_out, 1)
                elif kind == "qt":
                    dst = qT[8 * h // HP][:, 8 * h % HP:8 * h % HP + 8, t * P:(t + 1) * P]
                    nc.scalar.activation(dst, bank.bitcast(F16).rearrange("p (h m) -> p h m", m=P),
                                         ACT.Copy).then_inc(work_out, 1)
                else:
                    copy_out(0, t, 0)

            for q in range(2):
                ln_hi(0, q, FRONT_LN1 + q, 0, xa_hl[0])
            for j in range(W_Q, W_KV):
                split_w(j)
            w_next = W_KV
            for t in range(TT):
                early_out(("q", t, 0))
                if t + 1 < TT:
                    for q in range(2):
                        ln_hi(t + 1, q, FRONT_LN1 + 2 * (t + 1) + q, 0, xa_hl[0])
                if t == 0:
                    act.wait_ge(w_split, W_KV)
                if t >= 2:
                    for h in range(H1 // 8):
                        early_out(("qt", t - 2, h))
                if t >= 1:
                    q_high(t - 1)
                early_out(("q", t, 1))
                for _ in range(EARLY_SPLITS[t]):
                    split_w(w_next)
                    w_next += 1
                if t in (0, 2):
                    ctx_hi(t // 2, t // 2)
            early_out(("key", 0, 0))
            for h in range(H1 // 8):
                early_out(("qt", TT - 2, h))
            q_high(TT - 1)
            early_out(("key", 1, 0))
            key_high(0, 0)
            for h in range(H1 // 8):
                early_out(("qt", TT - 1, h))
            for n in range(2, NT):
                copy_out(0, n, 0)
                if n == 3:
                    key_high(0, 1)
                if n >= 4:
                    split_w(w_next)
                    w_next += 1

            def denominators_out(p, g):
                act.wait_ge(den_ready, p * GP + g + 1)
                nc.scalar.activation(group_den(g), ps[:, OUTS + g % 2, :], ACT.Copy).then_inc(den_out, 1)

            def stage(s, b, p):
                project = not (isinstance(s, int) and s + 1 >= STAGES)
                for u in range(UNITS):
                    n = s * UNITS + u
                    if isinstance(s, int) and s == 0 and u == 0:
                        act.wait_ge(w_split, W_END)
                    act.wait_ge(scores_ready, n + 1)
                    at_least(act, pv_done, s * (UNITS // 2) + (u // 2 - 1))
                    at_least(act, probs_summed, n - 3)
                    nc.scalar.activation(probs[u % 4], ps[:, SCORES + 2 * (u % 2):SCORES + 2 * (u % 2) + 2, :]
                                         .rearrange("p a n -> p (a n)"), ACT.Exp,
                                         scale=DH1 ** -0.5 / ACT_SCALE ** 2).then_inc(probs_ready, 1)
                    if u >= 1 and (due := denominators_due(s, u - 1, p)):
                        denominators_out(*due)
                    if isinstance(s, int) and s in (NCH, NCH + 1) and u in W_STEPS:
                        split_w(W_SA + (s - NCH) * 4 + W_STEPS.index(u))
                    if not project:
                        continue
                    if u == 1 and not (isinstance(s, int) and s + 2 >= STAGES):
                        ctx_hi(s + 2, b)
                    for k in range(NT):
                        if task_end[k] == u:
                            copy_out(s + 1, k, 1 - b)
                    for t in range(MT):
                        if task_end[t] + 3 == u:
                            key_high(s + 1, t)

            stages(act, stage)
            denominators_out(PASSES - 1, GP - 2)
            denominators_out(PASSES - 1, GP - 1)
            after_act(act, split_w, ln_hi)

        @block.vector
        def _(dve):
            step_no = [0]

            def step(ins):
                ins.then_inc(dve_step, 1)
                step_no[0] = step_no[0] + 1
                dve.wait_ge(dve_step, step_no[0])

            def rsqrt(v, cols, res):
                y, t = nt_y[:, 0:cols], nt_t[:, 0:cols]
                step(nc.vector.tensor_scalar(y.bitcast(I32), v.bitcast(I32), -0.5, RSQRT_MAGIC, ALU.mult, ALU.add))
                for k in range(NEWTON):
                    step(nc.vector.tensor_tensor(t, y, y, ALU.mult))
                    step(nc.vector.scalar_tensor_tensor(t, t, -0.5, v, ALU.mult, ALU.mult))
                    last = nc.vector.scalar_tensor_tensor(res if k == NEWTON - 1 else y, t, 1.5, y, ALU.add, ALU.mult)
                    if k < NEWTON - 1:
                        step(last)
                return last

            def split_w(j):
                src, hi, lo, slot = w_jobs[j]
                dve.wait_ge(w_hi_ready, j + 1)
                nc.vector.scalar_tensor_tensor(lo, slots[slot], W_SCALE, hi, ALU.mult, ALU.subtract).then_inc(w_split, 1)

            def ctx_lo(c, b):
                dve.wait_ge(ctx_hi_ready, c + 1)
                nc.vector.scalar_tensor_tensor(ctx_hl[b][1], ctx_f, ACT_SCALE, ctx_hl[b][0], ALU.mult,
                                               ALU.subtract).then_inc(ctx_split, 1)

            def ln_tile(t, ln, src, norm, front):
                for k in range(2):
                    step(nc.vector.bn_stats(bn[:, k, :], src[:, t, 512 * k:512 * k + 512]))
                step(nc.vector.bn_aggr(mv[:, t, :], bn[:, :, :]))
                step(nc.vector.tensor_scalar(nt_v[:, 0:1], mv[:, t, 1:2], 1e-5, None, ALU.add))
                step(rsqrt(nt_v[:, 0:1], 1, rs_ln[:, t:t + 1]))
                if t >= 2:
                    dve.wait_ge(front_ready, front + 2 * (t - 1))
                nc.vector.tensor_scalar(norm[t % 2], src[:, t], mv[:, t, 0:1], rs_ln[:, t:t + 1], ALU.subtract,
                                        ALU.mult).then_inc(normed, 1)

            def ln_lo(t, q, front, ln, hl):
                dve.wait_ge(ln_hi_ready, ln * 2 * TT + 2 * t + q + 1)
                at = (slice(None), slice(4 * q, 4 * q + 4), slice(t * P, (t + 1) * P))
                nc.vector.scalar_tensor_tensor(hl[1][at], ps[:, front % 4, :].rearrange("p (d n) -> p d n", n=P),
                                               ACT_SCALE, hl[0][at], ALU.mult, ALU.subtract).then_inc(front_free, 1)

            def ln_low(t, ln, hl, front):
                for q in range(2):
                    ln_lo(t, q, front + 2 * t + q, ln, hl)

            def key_stats(c, t):
                dve.wait_ge(key_sq_ready, c * MT + (t + 1))
                v = nt_v[:, 0:HP]
                step(nc.vector.reduce_sum(v, keys_sq[t], axis=AX_X))
                step(nc.vector.tensor_scalar(v, v, 1.0 / (DH1 * ACT_SCALE ** 2), 1e-6 / ACT_SCALE ** 2, ALU.mult, ALU.add))
                rsqrt(v, HP, rs_key[t][:, :]).then_inc(key_rs_ready, 1)

            def first_ln(t):
                dve.wait_ge(x_loaded[t], 16)
                ln_tile(t, 0, x_a, norm_a, FRONT_LN1)

            first_ln(0)
            ln_low(0, 0, xa_hl, FRONT_LN1)
            for j in range(W_Q, W_KV):
                split_w(j)
            first_ln(1)
            first_ln(2)
            ln_low(1, 0, xa_hl, FRONT_LN1)
            w_next = W_KV
            for t in range(TT):
                dve.wait_ge(q_sq_ready, t + 1)
                step(nc.vector.reduce_sum(nt_v[:, :], q_sq, axis=AX_X))
                step(nc.vector.tensor_scalar(nt_v[:, :], nt_v[:, :], 1.0 / (DH1 * ACT_SCALE ** 2), 1e-6 / ACT_SCALE ** 2,
                                             ALU.mult, ALU.add))
                if t >= 1:
                    dve.wait_ge(q_normed, t)
                rsqrt(nt_v[:, :], H1, rs_q[:, :]).then_inc(q_rs_ready, 1)
                if t + 3 < TT:
                    first_ln(t + 3)
                if t + 2 < TT:
                    ln_low(t + 2, 0, xa_hl, FRONT_LN1)
                for _ in range(EARLY_SPLITS[t]):
                    if t < TT - 1:
                        split_w(w_next)
                        w_next += 1
                if t in (0, 2):
                    ctx_lo(t // 2, t // 2)
                dve.wait_ge(q_hi, t + 1)
                nc.vector.tensor_tensor(q_stack[t % 2][:, :, 2:4, :],
                                        q_raw[t % 2].unsqueeze(2).to_broadcast([P, H1, 2, DH1]),
                                        q_stack[t % 2][:, :, 0:2, :], ALU.subtract).then_inc(q_stacked, 1)
            key_stats(0, 0)
            for _ in range(EARLY_SPLITS[TT - 1]):
                split_w(w_next)
                w_next += 1
            key_stats(0, 1)
            while w_next < W_END:
                split_w(w_next)
                w_next += 1
            steps0 = step_no[0]
            STEPS = MT * (3 + 3 * NEWTON - 1)

            def add_outs(count, p, g, bank, first):
                at_least(dve, pv_done, (count + 1) * MT)
                at_least(dve, outs_added, count)
                if first:
                    ins = nc.vector.tensor_copy(att[:, p * GP + g], ps[:, bank, :])
                else:
                    ins = nc.vector.tensor_tensor(att[:, p * GP + g], ps[:, bank, :], att[:, p * GP + g], ALU.add)
                ins.then_inc(outs_added, 1)

            def divide(p, g):
                n = p * GP + g
                dve.wait_ge(den_out, n + 1)
                dve.wait_ge(outs_added, ((p + 1) * NCH - 1) * GP + g + 1)
                nc.vector.reciprocal(group_den(g), group_den(g)).then_inc(den_inverted, 1)
                dve.wait_ge(den_inverted, n + 1)
                nc.vector.tensor_tensor(att[:, n], att[:, n], group_den(g), ALU.mult).then_inc(att_ready, 1)

            def stage(s, b, p):
                project = not (isinstance(s, int) and s + 1 >= STAGES)
                step_no[0] = s * STEPS + steps0
                first = first_of_pass(s)
                second = isinstance(s, int) and s % NCH == 1
                for u in range(UNITS):
                    g, t, head = unit(u)
                    n = s * UNITS + u
                    dve.wait_ge(probs_ready, n + 1)
                    at_least(dve, probs_summed, n - 1)
                    acc = prob_sum[:, head * N:(head + 2) * N]
                    if first and t == 0:
                        ins = nc.vector.tensor_copy(acc, probs[u % 4])
                    else:
                        ins = nc.vector.tensor_tensor(acc, acc, probs[u % 4], ALU.add)
                    ins.then_inc(probs_summed, 1)
                    if u % 4 == 1 and not (p == 0 and first and u == 1):
                        g = (u - 2) // 4 % GP
                        add_outs(s * GP + (u - 2) // 4, p - 1 if first and u == 1 else p, g, OUTS + g % 2, (first and u > 1) or (second and u == 1))
                    if u >= 3 and (due := denominators_due(s, u - 3, p)):
                        divide(*due)
                    if isinstance(s, int) and s in (NCH, NCH + 1) and u in W_STEPS:
                        split_w(W_SA + (s - NCH) * 4 + W_STEPS.index(u))
                    if not project:
                        continue
                    if u == 2 and not (isinstance(s, int) and s + 2 >= STAGES):
                        ctx_lo(s + 2, b)
                    for t in range(MT):
                        if task_end[t] + 1 == u:
                            key_stats(s + 1, t)
            stages(dve, stage)
            add_outs(STAGES * GP - 1, PASSES - 1, GP - 1, OUTS + (GP - 1) % 2, False)
            divide(PASSES - 1, GP - 2)
            divide(PASSES - 1, GP - 1)
            after_dve(dve, step, split_w, ln_tile, ln_low)

        @block.tensor
        def _(pe):
            def transpose_tokens(t, front0, norm, ln):
                pe.wait_ge(normed, ln * TT + t + 1)
                for q in range(2):
                    f = front0 + 2 * t + q
                    at_least(pe, front_free, f - 3)
                    for k in range(4):
                        d = 4 * q + k
                        last = nc.tensor.transpose(ps[:, f % 4, k * P:(k + 1) * P], norm[t % 2][:, d * P:(d + 1) * P],
                                                   ident[:, :])
                    last.then_inc(front_ready, 1)

            def split_product(dst, left, right, i, last_item):
                d, k = divmod(i, 3)
                a, b_ = ((0, 0), (0, 1), (1, 0))[k]
                return nc.tensor.matmul(dst, left[a](d), right[b_](d), start=(i == 0), stop=last_item)

            pe.wait_ge(ident_ready, 5)
            transpose_tokens(0, FRONT_LN1, norm_a, 0)
            pe.wait_ge(w_split, W_KV)
            for task in early:
                kind, t, h = task
                no = work_no[task]
                at_least(pe, work_out, no - 1)
                if kind == "q":
                    if h == 0:
                        pe.wait_ge(front_free, FRONT_LN1 + 2 * (t + 1))
                    left = [lambda d, v=v: v[:, d, t * P:(t + 1) * P] for v in xa_hl]
                    right = [lambda d, v=v: v[:, d, 512 * h:512 * h + 512] for v in wq]
                    for i in range(3 * DC):
                        last = split_product(ps[:, WORK + no % 2, :], left, right, i, i == 3 * DC - 1)
                elif kind == "qt":
                    if h == 0:
                        pe.wait_ge(q_stacked, t + 1)
                    for k in range(8):
                        last = nc.tensor.transpose(ps[:, WORK + no % 2, :].bitcast(F16)[:, k * P:(k + 1) * P],
                                                   q_stack[t % 2][:, 8 * h + k].rearrange("p s d -> p (s d)"), ident16[:, :])
                else:
                    if t == 0:
                        pe.wait_ge(w_split, W_KV2)
                        pe.wait_ge(ctx_split, 1)
                    left = [lambda d, v=v: v[:, d, t * P:(t + 1) * P] for v in ctx_hl[0]]
                    right = [lambda d, v=v: v[:, d, 0:KW] for v in wkv[0]]
                    for i in range(3 * DC):
                        last = split_product(ps[:, WORK + no % 2, :], left, right, i, i == 3 * DC - 1)
                last.then_inc(work_ready, 1)
                if kind == "q" and h == 0 and t + 1 < TT:
                    transpose_tokens(t + 1, FRONT_LN1, norm_a, 0)

            def chunk_item(c, b, p, item):
                n, i, ends = item
                kind, t, h = TASKS[n]
                bank = ps[:, WORK + TASK_BANK[n], :]
                if i == 0:
                    pe.wait_ge(work_out, c * NT + (W0 + TASK_FREE[n]))
                    if n == 0:
                        pe.wait_ge(ctx_split, c + 1)
                    if kind == "T" and h == 0:
                        pe.wait_ge(key_stacked, c * MT + (t + 1))
                if kind == "T":
                    ins = nc.tensor.transpose(bank.bitcast(F16)[:, i * P:(i + 1) * P],
                                              key_stack[t][:, 8 * h + i].rearrange("p s d -> p (s d)"), ident16[:, :])
                else:
                    w0 = 0 if kind == "K" else KW
                    left = [lambda d, v=v: v[:, d, t * P:(t + 1) * P] for v in ctx_hl[b]]
                    right = [lambda d, v=v: v[:, d, w0:w0 + KW] for v in wkv[p]]
                    ins = split_product(bank, left, right, i, ends)
                if ends:
                    ins.then_inc(work_ready, 1)

            def times_values(q, b, count, divided=0):
                g, t, head = unit(2 * q)
                if t == 0:
                    at_least(pe, outs_added, count - 1)
                    if divided:
                        pe.wait_ge(den_out, divided)
                for j in range(4):
                    last = nc.tensor.matmul(ps[32 * j:32 * j + 32, OUTS + g % 2, :],
                                            values[b][:, t, (head + j) * DH1:(head + j + 1) * DH1],
                                            probs[(2 * q + j // 2) % 4][:, j % 2 * N:(j % 2 + 1) * N],
                                            start=(t == 0), stop=(t == MT - 1))
                last.then_inc(pv_done, 1)

            def denominators(p, g):
                done = (p + 1) * NCH
                pe.wait_ge(probs_summed, done * UNITS - UNITS + 4 * g + 4)
                pe.wait_ge(outs_added, done * GP - GP + g + 1)
                for j in range(4):
                    head = 4 * g + j
                    last = nc.tensor.matmul(ps[32 * j:32 * j + 32, OUTS + g % 2, :], ones[:, :],
                                            prob_sum[:, head * N:(head + 1) * N], start=True, stop=True)
                last.then_inc(den_ready, 1)

            for its in per_step:
                for it in its:
                    if TASKS[it[0]][0] != "K":
                        chunk_item(0, 0, 0, it)

            def stage(s, b, p):
                project = not (isinstance(s, int) and s + 1 >= STAGES)
                for u in range(UNITS):
                    g, t, head = unit(u)
                    n = s * UNITS + u
                    if u == 0:
                        pe.wait_ge(work_out, s * NT + (W0 + 4))
                    if u == 2:
                        pe.wait_ge(work_out, s * NT + (W0 + 7))
                    if u == 5:
                        pe.wait_ge(work_out, s * NT + (W0 + 8))
                    at_least(pe, probs_ready, n - 1)
                    for k in range(2):
                        last = nc.tensor.matmul(ps[:, SCORES + 2 * (u % 2) + k, :],
                                                kT[b][:, head + k, t * P:(t + 1) * P], qT[p][:, head + k, :],
                                                start=True, stop=True)
                    last.then_inc(scores_ready, 1)
                    if u % 2 and u >= 3:
                        g = (u - 3) // 4
                        divided = p * GP + g - 1 if last_of_pass(s) and g >= 2 or first_of_pass(s) and p and g < 2 else 0
                        times_values((u - 3) // 2, b, s * GP + g, divided)
                    elif u == 1 and not (p == 0 and first_of_pass(s)):
                        times_values(UNITS // 2 - 1, 1 - b, s * GP - 1)
                    if due := denominators_due(s, u, p):
                        denominators(*due)
                    if project:
                        if u == 0 and last_of_pass(s):
                            pe.wait_ge(w_split, W_END)
                        for it in per_step[u]:
                            chunk_item(s + 1, 1 - b, pass_of_next(s, p), it)
            stages(pe, stage)
            pe.wait_ge(probs_ready, STAGES * UNITS)
            times_values(UNITS // 2 - 1, 1, STAGES * GP - 1)
            denominators(PASSES - 1, GP - 2)
            denominators(PASSES - 1, GP - 1)
            after_pe(pe, transpose_tokens, split_product)


def laid_out(inputs):
    import numpy as np

    def tiles(w, cols):
        d, c = w.shape
        return w.reshape(d // 128, 128, c // cols, cols).transpose(2, 1, 0, 3)

    a = {k: np.asarray(v) for k, v in inputs.items()}
    wkv = np.concatenate([a["L0_xattn_Wk"], a["L0_xattn_Wv"]], 0)
    wkv = wkv.reshape(2, 512, 2, wkv.shape[1]).transpose(3, 0, 2, 1)
    return {
        "x": a["x"][0],
        "ctx_t": tiles(a["ctx_2048"][0].T, 256),
        "wq_t": a["L0_xattn_Wq"].T,
        "wkv_t": wkv.reshape(wkv.shape[0], -1),
        "wqkv_t": a["L0_attn_Wqkv"].T,
        "wproj_t": a["L0_attn_Wproj"].T,
        "wg_t": tiles(a["L0_ffn_wq_gate"].T, 128),
        "wu_t": tiles(a["L0_ffn_wq_up"].T, 128),
        "wd_t": a["L0_ffn_wq_down"].T,
        "s_gate": a["L0_ffn_s_gate"].reshape(-1, 128).T,
        "s_up": a["L0_ffn_s_up"].reshape(-1, 128).T,
        "s_down": a["L0_ffn_s_down"].reshape(1, -1),
    }


def kernel(**inputs):
    import numpy as np
    import concourse.bacc as bacc
    from concourse import mybir as mb
    from concourse.bass_utils import run_bass_kernel_spmd

    nc = bacc.Bacc("TRN2", target_bir_lowering=False, num_devices=1, dynamic_dma_scratch_size=1024)
    arrays, args = {}, []
    for name, a in laid_out(inputs).items():
        a = np.ascontiguousarray(a)
        arrays["in_" + name] = a
        args.append(nc.dram_tensor("in_" + name, a.shape, mb.dt.from_np(a.dtype), kind="ExternalInput").ap())
    shape = tuple(np.asarray(inputs["x"]).shape)
    args.append(nc.dram_tensor("out_0", shape[1:], mb.dt.float32, kind="ExternalOutput").ap())
    build_perceiver(nc, *args)
    r = run_bass_kernel_spmd(nc, [arrays], core_ids=[0])
    return np.asarray(r.results[0]["out_0"]).reshape(shape)
```

```python
from contextlib import ExitStack

import concourse.bass as bass
from concourse import mybir

F32 = mybir.dt.float32
F16 = mybir.dt.float16
I32 = mybir.dt.int32
ALU = mybir.AluOpType
ACT = mybir.ActivationFunctionType
AX_X = mybir.AxisListType.X

P = 128
ACT_SCALE = 64.0
W_SCALE = 1024.0
HID_SCALE = 16.0
PROD = ACT_SCALE * W_SCALE
RSQRT_MAGIC = 1597463007.0
NEWTON = 3
SPLIT_TERMS = ((0, 0), (0, 1), (1, 0))


def build_perceiver(nc, x, ctx_t, wq_t, wkv_t, wqkv_t, wproj_t, wg_t, wu_t, wd_t, s_gate, s_up, s_down, out):
    N, D = x.shape
    CM = ctx_t.shape[3]
    M = ctx_t.shape[0] * CM
    HID = wd_t.shape[0]
    H1, DH1 = 32, D // 32
    H2, DH2 = 16, D // 16
    TT = N // P
    DC = D // P
    MT = CM // P
    NCH = M // CM
    PASSES = 2
    HP = H1 // PASSES
    GP = HP // 4
    UNITS = GP * MT * 2
    STAGES = PASSES * NCH
    HT = HID // P
    KW = HP * DH1
    assert N == 512 and D == 1024 and KW == 512 and M % CM == 0 and HID % P == 0

    with ExitStack() as stack:
        def sb(name, shape, dt):
            return stack.enter_context(nc.sbuf_tensor(name, shape, dt))

        def sem(name):
            return stack.enter_context(nc.semaphore(name))

        KB = 256
        arena = sb("arena", [P, 220 * KB], F32)

        def region(at_kb, kb, dt=F32):
            r = arena[:, int(at_kb * KB):int((at_kb + kb) * KB)]
            return r if dt == F32 else r.bitcast(dt)

        def pair(at_kb, kb, cols):
            v = region(at_kb, kb, F16).rearrange("p (s d c) -> p s d c", s=2, c=cols)
            return v[:, 0], v[:, 1]

        wkv = [pair(32 * p, 32, 2 * KW) for p in range(PASSES)]
        qT = [region(64 + 16 * p, 16, F16).rearrange("p (h n) -> p h n", n=N) for p in range(PASSES)]
        kT = [region(96 + 8 * b, 8, F16).rearrange("p (h m) -> p h m", m=CM) for b in range(2)]
        values = [region(112 + 4 * b, 4).rearrange("p (t c) -> p t c", c=KW) for b in range(2)]
        ctx_f = region(120, 8).rearrange("p (d m) -> p d m", m=CM)
        ctx_hl = [pair(128 + 8 * b, 8, CM) for b in range(2)]
        keys = [region(144 + 2 * t, 2).rearrange("p (h d) -> p h d", d=DH1) for t in range(MT)]
        key_stack = [region(148 + 4 * t, 4, F16).rearrange("p (h s d) -> p h s d", s=4, d=DH1) for t in range(MT)]
        keys_sq = [region(148 + 4 * t, 2).rearrange("p (h d) -> p h d", d=DH1) for t in range(MT)]
        probs = [region(156 + 4 * b, 4) for b in range(4)]
        prob_sum = region(172, 32)
        att = region(204, 16).rearrange("p (g n) -> p g n", n=N)
        x_a = region(166, 16).rearrange("p (t c) -> p t c", c=D)
        xa_hl = pair(182, 16, N)
        norm_a = [region(198 + 4 * b, 4) for b in range(2)]
        q_raw = [region(206 + 4 * b, 4).rearrange("p (h d) -> p h d", d=DH1) for b in range(2)]
        q_sq = region(150, 4).rearrange("p (h d) -> p h d", d=DH1)
        q_stack = [region(96 + 8 * b, 8, F16).rearrange("p (h s d) -> p h s d", s=4, d=DH1) for b in range(2)]
        wq = pair(32, 32, D)
        rden = sb("rden", [P, PASSES, TT, HP], F32)
        x1 = region(64, 16).rearrange("p (t c) -> p t c", c=D)
        wqkv = [pair(at_, 32, D) for at_ in (0, 32, 166)]
        wproj = pair(0, 32, D)
        xb_hl = pair(80, 16, N)
        norm_b = [region(128 + 4 * b, 4) for b in range(2)]
        q2T = region(96, 16).rearrange("p (c n) -> p c n", n=N)
        k2T = region(144, 16).rearrange("p (c n) -> p c n", n=N)
        v2 = region(198, 16).rearrange("p (t c) -> p t c", c=D)
        sa_p = [region(136 + 2 * b, 2) for b in range(4)]
        sa_pT = [region(32 + 8 * b, 8).rearrange("p (k n) -> p k n", n=N) for b in range(2)]
        sa_out = pair(48, 16, N)
        mask = region(164, 2)
        sa_max, sa_neg, sa_sum, sa_inv = [region(160 + 0.25 * k, 0.25) for k in range(4)]
        w_stage = [region(112 + 4 * b, 4) for b in range(4)]
        ring = [[pair(166 + 8 * r + 4 * m, 4, P) for m in range(2)] for r in range(4)]
        w_down = [pair(4 * j if j < 16 else 140 + 4 * (j - 16), 4, D) for j in range(HT)]
        hid_at = [96 + 2 * j for j in range(8)] + [128 + 2 * j for j in range(6)] + [198 + 2 * j for j in range(8)]
        hid = [pair(a, 2, N) for a in hid_at]
        s_down_b = region(214, 4)
        y = region(166, 16).rearrange("p (t c) -> p t c", c=D)
        silu_b = [region(164, 2), region(218, 2)]
        sg = sb("sg", [P, HT], F32)
        su = sb("su", [P, HT], F32)
        slots = [region(a, 4) for a in (214, 158, 162, 116, 120, 124, 64, 68, 0, 4, 8, 12, 16, 20, 24, 28)]

        code_max = sb("code_max", [P, 3 * HT], F32)
        row_max = sb("row_max", [P, 2], F32)
        large = sb("large", [1, 1], I32)
        ident = sb("ident", [P, P], F32)
        ident16 = sb("ident16", [P, P], F16)
        ones = sb("ones", [P, DH1], F32)
        bn = sb("bn", [P, 2, 6], F32)
        mv = sb("mv", [P, TT, 2], F32)
        nt_v = sb("nt_v", [P, 32], F32)
        nt_y = sb("nt_y", [P, 32], F32)
        nt_t = sb("nt_t", [P, 32], F32)
        rs_key = [sb(f"rs_key{t}", [P, HP], F32) for t in range(MT)]
        rs_q = sb("rs_q", [P, H1], F32)
        rs_ln = sb("rs_ln", [P, TT], F32)

        ps = stack.enter_context(nc.psum_tensor("ps", [P, 8, 512], F32))
        SCORES, OUTS, WORK = 0, 4, 6

        ident_ready = sem("ident_ready")
        x_loaded = [sem(f"x_loaded{t}") for t in range(TT)]
        ctx_loaded = sem("ctx_loaded")
        ctx_hi_ready = sem("ctx_hi_ready")
        ctx_split = sem("ctx_split")
        w_loaded = [sem(f"w_loaded{s}") for s in range(len(slots))]
        w_hi_ready = sem("w_hi_ready")
        w_split = sem("w_split")
        dve_step = sem("dve_step")
        normed = sem("normed")
        front_ready = sem("front_ready")
        ln_hi_ready = sem("ln_hi_ready")
        front_free = sem("front_free")
        work_ready = sem("work_ready")
        work_out = sem("work_out")
        q_sq_ready = sem("q_sq_ready")
        q_rs_ready = sem("q_rs_ready")
        q_normed = sem("q_normed")
        q_hi = sem("q_hi")
        q_stacked = sem("q_stacked")
        key_sq_ready = sem("key_sq_ready")
        key_rs_ready = sem("key_rs_ready")
        key_normed = sem("key_normed")
        key_hi = sem("key_hi")
        key_stacked = sem("key_stacked")
        scores_ready = sem("scores_ready")
        probs_ready = sem("probs_ready")
        probs_summed = sem("probs_summed")
        pv_done = sem("pv_done")
        outs_added = sem("outs_added")
        den_ready = sem("den_ready")
        den_out = sem("den_out")
        den_turned = sem("den_turned")
        den_inverted = sem("den_inverted")

        x_again = sem("x_again")
        sa_scores = sem("sa_scores")
        sa_masked = sem("sa_masked")
        sa_exp = sem("sa_exp")
        sa_norm = sem("sa_norm")
        sa_turned = sem("sa_turned")
        sa_turned_out = sem("sa_turned_out")
        sa_pv = sem("sa_pv")
        sa_out_hi = sem("sa_out_hi")
        sa_out_split = sem("sa_out_split")
        mask_ready = sem("mask_ready")
        proj_ready = sem("proj_ready")
        proj_added = sem("proj_added")
        scales_loaded = sem("scales_loaded")
        scales_ready = sem("scales_ready")
        codes_checked = sem("codes_checked")
        checks_turned = sem("checks_turned")
        large_ready = sem("large_ready")

        class FfnSemaphores:
            def __init__(self, way):
                self.loaded = [sem(f"f_loaded{b}_{way}") for b in range(4)]
                self.value = sem("f_value_" + way)
                self.hi = sem("f_hi_" + way)
                self.split = sem("f_split_" + way)
                self.gu_ready = sem("gu_ready_" + way)
                self.silu_ready = sem("silu_ready_" + way)
                self.hid_ready = sem("hid_ready_" + way)
                self.hid_hi = sem("hid_hi_" + way)
                self.hid_split = sem("hid_split_" + way)
                self.down_ready = sem("down_ready_" + way)
                self.down_scaled = sem("down_scaled_" + way)
                self.down_out = sem("down_out_" + way)
                self.stored = sem("stored_" + way)

        short, long = FfnSemaphores("short"), FfnSemaphores("long")

        early = []
        for t in range(TT):
            early.append(("q", t, 0))
            if t >= 2:
                early += [("qt", t - 2, b) for b in range(H1 // 8)]
            early.append(("q", t, 1))
        for t in range(MT):
            early.append(("key", t, 0))
            early += [("qt", TT - 2 + t, b) for b in range(H1 // 8)]
        work_no = {task: n for n, task in enumerate(early)}
        W0 = len(early) - MT

        def key_no(c, t):
            return work_no["key", t, 0] if isinstance(c, int) and c == 0 else c * NT + (W0 + t)

        TASKS = [("K", 0, 0), ("K", 1, 0), ("T", 0, 0), ("T", 0, 1), ("V", 0, 0), ("T", 1, 0), ("T", 1, 1), ("V", 1, 0)]
        TASK_BANK = [0, 1, 1, 1, 0, 0, 0, 1]
        TASK_FREE = [-1, 0, 2, 3, 1, 5, 6, 4]
        NT = len(TASKS)
        products = [(TASKS.index((kind, t, 0)), i, i == 3 * DC - 1) for kind in "KV" for t in range(MT) for i in range(3 * DC)]
        PER_STEP = len(products) // UNITS
        T_STEPS = {9: ("T", 0, 0), 10: ("T", 0, 1), 13: ("T", 1, 0), 14: ("T", 1, 1)}
        per_step = [products[u * PER_STEP:(u + 1) * PER_STEP] +
                    [(TASKS.index(T_STEPS[u]), i, i == 7) for i in range(8) if u in T_STEPS] for u in range(UNITS)]
        task_end = {it[0]: u for u, its in enumerate(per_step) for it in its if it[2]}
        assert sorted(task_end, key=task_end.get) == list(range(NT))

        FRONT_LN1 = 0
        FRONT_BACK = FRONT_LN1 + 2 * TT
        FRONT_LN2 = FRONT_BACK + 2 * TT
        FRONT_LN3 = FRONT_LN2 + 2 * TT

        w_jobs = []
        for d in range(DC):
            w_jobs.append((wq_t[d * P:(d + 1) * P, :], wq[0][:, d], wq[1][:, d], 8 + d))
        for p in range(PASSES):
            for d in range(DC):
                w_jobs.append((wkv_t[d * P:(d + 1) * P, p * 1024:(p + 1) * 1024], wkv[p][0][:, d], wkv[p][1][:, d],
                               len(w_jobs) % 4))
        W_Q, W_KV, W_KV2, W_END = 0, DC, 2 * DC, 3 * DC
        W_SA = W_END
        SA_PARTS = (2, 1, 0)
        for k, part in enumerate(SA_PARTS):
            for d in range(DC):
                w_jobs.append((wqkv_t[d * P:(d + 1) * P, part * D:(part + 1) * D], wqkv[k][0][:, d],
                               wqkv[k][1][:, d], 6 + d % 2 if k == 0 else (4, 5, 0)[(len(w_jobs) - W_SA - DC) % 3]))
        W_PROJ = len(w_jobs)
        for d in range(DC):
            w_jobs.append((wproj_t[d * P:(d + 1) * P, :], wproj[0][:, d], wproj[1][:, d], (4, 5, 0)[(len(w_jobs) - W_SA - DC) % 3]))
        slot_use = []
        for j, job in enumerate(w_jobs):
            slot_use.append(sum(1 for k in w_jobs[:j] if k[3] == job[3]))
        slot_before = [max([k for k in range(j) if w_jobs[k][3] == w_jobs[j][3]], default=None) for j in range(len(w_jobs))]

        def unit(u):
            g, rest = divmod(u, 2 * MT)
            t, pr = divmod(rest, 2)
            return g, t, 4 * g + 2 * pr

        ctx_v = ctx_t.rearrange("c p d m -> c p (d m)")
        x_v = x.rearrange("(t p) c -> t p c", p=P)

        def at_least(eng, s, n):
            if not isinstance(n, int) or n > 0:
                eng.wait_ge(s, n)

        def stages(eng, emit):
            for p in range(PASSES):
                base = p * NCH
                emit(base, 0, p)
                emit(base + 1, 1, p)
                with eng.Fori(0, (NCH - 4) // 2) as i:
                    for b in range(2):
                        emit(i * 2 + (base + 2 + b), b, p)
                emit(base + NCH - 2, 0, p)
                emit(base + NCH - 1, 1, p)

        def last_of_pass(s):
            return isinstance(s, int) and s % NCH == NCH - 1

        def first_of_pass(s):
            return isinstance(s, int) and s % NCH == 0

        def denominators_due(s, u, p):
            if u % 4 == 0:
                if last_of_pass(s) and u >= 8:
                    return p, (u - 8) // 4
                if first_of_pass(s) and p and u < 4 * (GP - 2):
                    return p - 1, (u + 4 * GP - 8) // 4
            return None

        def group_den(g):
            return prob_sum[:, 4 * g * N:(4 * g + 1) * N]

        def pass_of_next(s, p):
            return p + 1 if last_of_pass(s) else p

        EARLY_SPLITS = (2, 3, 3, 4)
        W_STEPS = (4, 7, 10, 13)

        W1 = W0 + NT * STAGES
        SA_FIRST = 2 * DC + 1
        SA_BANKS = 3
        Q_PER_UNIT = 4
        SA_UNITS = H2 * TT
        SA_LAG = 3

        f_jobs = [(m, j) for j in range(4) for m in ("gate", "up")]
        for j in range(HT):
            f_jobs.append(("down", j))
            if j + 4 < HT:
                f_jobs += [("gate", j + 4), ("up", j + 4)]
        f_no = {job: n for n, job in enumerate(f_jobs)}
        F_AHEAD = 8
        CODE_SCALE = 2.0 ** -14
        GU_SCALE = 1.0 / (CODE_SCALE * ACT_SCALE)

        SMALL_CODE = 2.0 ** 11 - 128

        def take_long_way(eng):
            eng.wait_ge(large_ready, 1)
            return eng.value_load(large[0:1, 0:1], min_val=0, max_val=1) != 0

        def f_dest(job):
            m, j = job
            if m == "down":
                return [v.rearrange("p a c -> p (a c)") for v in w_down[j]]
            return [v.rearrange("p a c -> p (a c)") for v in ring[j % 4][m == "up"]]

        def f_turn(j):
            return [f_no[job] for job in [("down", j), ("gate", j + 4), ("up", j + 4)] if job in f_no]

        def self_attention_and_ffn_sp(sp, load_w):
            sp.wait_ge(ctx_split, STAGES)
            for j in range(W_SA + DC, len(w_jobs)):
                if j == W_SA + DC + 2:
                    sp.wait_ge(front_ready, FRONT_LN2)
                load_w(j)
            sp.dma_start(sg[:, :], s_gate).then_inc(scales_loaded, 16)
            sp.dma_start(su[:, :], s_up).then_inc(scales_loaded, 16)
            sp.wait_ge(w_split, len(w_jobs))
            sp.dma_start(s_down_b, s_down.to_broadcast([P, D])).then_inc(scales_loaded, 16)
            def f_loads(way):
                for n, (m, j) in enumerate(f_jobs):
                    src = {"gate": lambda: wg_t[j].rearrange("p d c -> p (d c)"),
                           "up": lambda: wu_t[j].rearrange("p d c -> p (d c)"),
                           "down": lambda: wd_t[j * P:(j + 1) * P, :]}[m]()
                    if way is short:
                        at_least(sp, way.hi, n - 3)
                        at_least(sp, codes_checked, n - 3)
                    else:
                        at_least(sp, way.split, n - 3)
                    sp.dma_start(w_stage[n % 4].bitcast(I32), src).then_inc(way.loaded[n % 4], 16)

            def stores(way):
                for t in range(TT):
                    for h in range(2):
                        sp.wait_ge(way.down_out, 2 * t + h + 1)
                        sp.dma_start(out[t * P:(t + 1) * P, 512 * h:512 * h + 512], y[:, t, 512 * h:512 * h + 512])\
                            .then_inc(way.stored, 16)

            f_loads(short)
            condition = take_long_way(sp)
            stores(short)
            sp.wait_ge(short.stored, 16 * 2 * TT)
            with sp.If(condition):
                f_loads(long)
                stores(long)
                sp.wait_ge(long.stored, 16 * 2 * TT)

        def self_attention_and_ffn_pool(pool):
            pool.wait_ge(pv_done, STAGES * UNITS // 2)
            pool.wait_ge(probs_summed, STAGES * UNITS)
            nc.gpsimd.memset(mask, 0.0).then_inc(mask_ready, 1)
            pool.wait_ge(mask_ready, 1)
            diagonal = mask[:, 3 * P:4 * P]
            nc.gpsimd.affine_select(out=diagonal, in_=diagonal, compare_op=ALU.is_ge, fill=-1e30, base=0,
                                    pattern=[[-1, P]], channel_multiplier=1).then_inc(mask_ready, 1)
            def hid_low(way):
                for j in range(HT):
                    pool.wait_ge(way.hid_hi, j + 1)
                    nc.gpsimd.tensor_tensor(hid[j][1][:, 0], silu_b[j % 2], hid[j][0][:, 0],
                                            ALU.subtract).then_inc(way.hid_split, 1)

            hid_low(short)
            with pool.If(take_long_way(pool)):
                hid_low(long)

        def self_attention_and_ffn_act(act, split_w, ln_hi):
            for q in range(2):
                ln_hi(0, q, FRONT_LN2 + q, 1, xb_hl[0])
            def projection_out(n, bank):
                k, c = divmod(n, DC)
                act.wait_ge(work_ready, W1 + n + 1)
                dst = (v2[:, c // 2, 512 * (c % 2):512 * (c % 2) + 512], k2T[:, c], q2T[:, c])[k]
                nc.scalar.activation(dst, ps[:, bank, :], ACT.Copy, scale=1.0 / PROD).then_inc(work_out, 1)

            for n in range(SA_FIRST):
                projection_out(n, WORK + n % 2)
                if n % 2 == 0 and n // 2 + 1 < TT:
                    for q in range(2):
                        ln_hi(n // 2 + 1, q, FRONT_LN2 + n + 2 + q, 1, xb_hl[0])
                if n < 2 * TT:
                    split_w(W_SA + DC + 2 * n)
                    split_w(W_SA + DC + 2 * n + 1)
                elif n < 2 * DC:
                    split_w(W_PROJ + n - DC)
            for k in range(SA_UNITS + 9):
                if k < SA_UNITS:
                    L = (k % TT + 1) * P
                    act.wait_ge(sa_masked, k + 1)
                    at_least(act, sa_turned, k - 3)
                    nc.scalar.activation(sa_p[k % 4][:, 0:L], ps[:, k % SA_BANKS, 0:L], ACT.Exp, bias=sa_neg[:, k:k + 1],
                                         scale=DH2 ** -0.5, accum_out=sa_sum[:, k:k + 1]).then_inc(sa_exp, 1)
                    if k % 8 == 24 // Q_PER_UNIT and k // 8 + 1 < DC:
                        projection_out(2 * DC + 1 + k // 8, SA_BANKS)
                m = k - SA_LAG
                if 0 <= m < SA_UNITS:
                    h, t = divmod(m, TT)
                    act.wait_ge(sa_turned, m + 1)
                    at_least(act, sa_pv, h - 1)
                    nc.scalar.activation(sa_pT[h % 2][:, 0:t + 1, t * P:(t + 1) * P],
                                         ps[:, WORK + m % 2, 0:(t + 1) * P].rearrange("p (k n) -> p k n", n=P),
                                         ACT.Copy).then_inc(sa_turned_out, 1)
                if k >= 16 and k % 8 == 0 or k == SA_UNITS + 8:
                    i = k // 8 - 2
                    act.wait_ge(sa_pv, 2 * i + 2)
                    nc.scalar.activation(sa_out[0][:, i], ps[:, OUTS + i % 2, :], ACT.Copy,
                                         scale=ACT_SCALE).then_inc(sa_out_hi, 1)

            def f_high(n, way):
                if way is short:
                    act.wait_ge(way.loaded[n % 4], 16 * (n // 4 + 1))
                    nc.scalar.activation(f_dest(f_jobs[n])[0], w_stage[n % 4].bitcast(I32), ACT.Copy, scale=CODE_SCALE,
                                         bias=-128.0 * CODE_SCALE).then_inc(way.hi, 1)
                else:
                    act.wait_ge(way.value, n + 1)
                    nc.scalar.activation(f_dest(f_jobs[n])[0], w_stage[n % 4], ACT.Copy).then_inc(way.hi, 1)

            def gate_up(way):
                for j in range(HT + 1):
                    if j < HT:
                        act.wait_ge(way.gu_ready, 2 * j + 1)
                        at_least(act, way.hid_split, j - 1)
                        nc.scalar.activation(silu_b[j % 2], ps[:, (WORK, OUTS)[j % 2], :], ACT.Silu,
                                             scale=sg[:, j:j + 1]).then_inc(way.silu_ready, 1)
                    if j >= 1:
                        act.wait_ge(way.hid_ready, j)
                        nc.scalar.activation(hid[j - 1][0][:, 0], silu_b[(j - 1) % 2], ACT.Copy).then_inc(way.hid_hi, 1)
                    if j < HT:
                        act.wait_ge(way.gu_ready, 2 * j + 2)
                        for n in f_turn(j):
                            f_high(n, way)

            for n in range(F_AHEAD):
                f_high(n, short)
                if n >= 2 and n % 2 == 0:
                    for q in range(2):
                        ln_hi(n // 2 - 1, q, FRONT_LN3 + n - 2 + q, 2, xb_hl[0])
            for q in range(2):
                ln_hi(TT - 1, q, FRONT_LN3 + 2 * (TT - 1) + q, 2, xb_hl[0])
            act.wait_ge(scales_ready, 1)
            gate_up(short)
            with act.If(take_long_way(act)):
                for n in range(F_AHEAD):
                    f_high(n, long)
                gate_up(long)

        def self_attention_and_ffn_dve(dve, step, split_w, ln_tile, ln_low):
            dve.wait_ge(x_again, 16)
            dve.wait_ge(den_inverted, PASSES * GP)
            for k in range(2 * TT):
                q, t = divmod(k, TT)
                dve.wait_ge(front_ready, FRONT_BACK + k + 1)
                xs = x1[:, t, 512 * q:512 * q + 512]
                bank = ps[:, (FRONT_BACK + k) % 4, :]
                heads = bank.rearrange("p (h d) -> p h d", d=DH1)
                step(nc.vector.tensor_tensor(heads, heads, rden[:, q, t, :].unsqueeze(2).to_broadcast([P, HP, DH1]), ALU.mult))
                nc.vector.tensor_tensor(xs, bank, xs, ALU.add).then_inc(front_free, 1)
                if (q, t) == (1, 0):
                    dve.wait_ge(front_free, FRONT_BACK + TT + 1)
                    ln_tile(0, 1, x1, norm_b, FRONT_LN2)
            dve.wait_ge(front_free, FRONT_BACK + 2 * TT)
            ln_low(0, 1, xb_hl, FRONT_LN2)
            ln_tile(1, 1, x1, norm_b, FRONT_LN2)
            for n in range(2 * DC):
                if n % 2 == 0 and n // 2 + 2 < TT:
                    ln_tile(n // 2 + 2, 1, x1, norm_b, FRONT_LN2)
                if n % 2 == 0 and n // 2 + 1 < TT:
                    ln_low(n // 2 + 1, 1, xb_hl, FRONT_LN2)
                if n < 2 * TT:
                    split_w(W_SA + DC + 2 * n)
                    split_w(W_SA + DC + 2 * n + 1)
                else:
                    split_w(W_PROJ + n - DC)
            dve.wait_ge(mask_ready, 2)
            for k in range(SA_UNITS + 9):
                if k < SA_UNITS:
                    L = (k % TT + 1) * P
                    s_ = ps[:, k % SA_BANKS, 0:L]
                    dve.wait_ge(sa_scores, k + 1)
                    step(nc.vector.tensor_tensor_reduce(out=s_, in0=s_, in1=mask[:, 4 * P - L:4 * P], scale=1.0, scalar=-3e38,
                                                        op0=ALU.add, op1=ALU.max, accum_out=sa_max[:, k:k + 1]))
                    nc.vector.tensor_scalar(sa_neg[:, k:k + 1], sa_max[:, k:k + 1], -(DH2 ** -0.5), None, ALU.mult)\
                        .then_inc(sa_masked, 1)
                if 1 <= k <= SA_UNITS:
                    m = k - 1
                    L = (m % TT + 1) * P
                    dve.wait_ge(sa_exp, m + 1)
                    step(nc.vector.reciprocal(sa_inv[:, m:m + 1], sa_sum[:, m:m + 1]))
                    nc.vector.tensor_scalar(sa_p[m % 4][:, 0:L], sa_p[m % 4][:, 0:L], sa_inv[:, m:m + 1], None,
                                            ALU.mult).then_inc(sa_norm, 1)
                if k >= 16 and k % 8 == 0 or k == SA_UNITS + 8:
                    i = k // 8 - 2
                    dve.wait_ge(sa_out_hi, i + 1)
                    nc.vector.scalar_tensor_tensor(sa_out[1][:, i], ps[:, OUTS + i % 2, :], ACT_SCALE, sa_out[0][:, i],
                                                   ALU.mult, ALU.subtract).then_inc(sa_out_split, 1)

            def f_check(n):
                dve.wait_ge(short.loaded[n % 4], 16 * (n // 4 + 1))
                nc.vector.tensor_reduce(code_max[:, n:n + 1], w_stage[n % 4].bitcast(I32), AX_X, ALU.max,
                                        apply_absolute_value=True).then_inc(codes_checked, 1)

            def f_float(n):
                dve.wait_ge(long.loaded[n % 4], 16 * (n // 4 + 1))
                nc.vector.tensor_scalar(w_stage[n % 4], w_stage[n % 4].bitcast(I32), -128.0, CODE_SCALE, ALU.add,
                                        ALU.mult).then_inc(long.value, 1)

            def f_low(n):
                hi, lo = f_dest(f_jobs[n])
                dve.wait_ge(long.hi, n + 1)
                nc.vector.tensor_tensor(lo, w_stage[n % 4], hi, ALU.subtract).then_inc(long.split, 1)

            def hid_value(j, way):
                dve.wait_ge(way.silu_ready, j + 1)
                dve.wait_ge(way.gu_ready, 2 * j + 2)
                nc.vector.scalar_tensor_tensor(silu_b[j % 2], ps[:, (WORK, OUTS)[j % 2] + 1, :], su[:, j:j + 1],
                                               silu_b[j % 2], ALU.mult, ALU.mult).then_inc(way.hid_ready, 1)

            def outputs(way):
                for k in range(2 * TT):
                    t, h = divmod(k, 2)
                    b = ps[:, k % 4, :]
                    at = (slice(None), t, slice(512 * h, 512 * h + 512))
                    dve.wait_ge(way.down_ready, k + 1)
                    nc.vector.tensor_tensor(b, b, s_down_b[:, 512 * h:512 * h + 512], ALU.mult).then_inc(way.down_scaled, 1)
                    dve.wait_ge(way.down_scaled, k + 1)
                    nc.vector.tensor_tensor(y[at], b, x1[at], ALU.add).then_inc(way.down_out, 1)

            dve.wait_ge(scales_loaded, 48)
            step(nc.vector.tensor_scalar(su[:, :], su[:, :], GU_SCALE * HID_SCALE, None, ALU.mult))
            step(nc.vector.tensor_scalar(s_down_b, s_down_b, 1.0 / (CODE_SCALE * HID_SCALE), None, ALU.mult))
            nc.vector.tensor_scalar(sg[:, :], sg[:, :], GU_SCALE, None, ALU.mult).then_inc(scales_ready, 1)
            for k in range(2 * TT):
                t, h = divmod(k, 2)
                dve.wait_ge(proj_ready, k + 1)
                xs = x1[:, t, 512 * h:512 * h + 512]
                nc.vector.scalar_tensor_tensor(xs, ps[:, WORK + k % 2, :], 1.0 / PROD, xs, ALU.mult,
                                               ALU.add).then_inc(proj_added, 1)
                if h == 1:
                    dve.wait_ge(proj_added, k + 1)
                    ln_tile(t, 2, x1, norm_b, FRONT_LN3)
                f_check(k)
                if t >= 1 and h == 0:
                    ln_low(t - 1, 2, xb_hl, FRONT_LN3)
            ln_low(TT - 1, 2, xb_hl, FRONT_LN3)
            for j in range(HT):
                hid_value(j, short)
                for n in f_turn(j):
                    f_check(n)
            dve.wait_ge(codes_checked, len(f_jobs))
            nc.vector.reduce_max(row_max[:, 0:1], code_max[:, :], axis=AX_X).then_inc(codes_checked, 1)
            dve.wait_ge(checks_turned, 1)
            step(nc.vector.reduce_max(row_max[0:1, 1:2], ps[0:1, WORK, 0:P], axis=AX_X))
            nc.vector.tensor_scalar(large[:, :], row_max[0:1, 1:2], SMALL_CODE, None, ALU.is_gt).then_inc(large_ready, 1)
            outputs(short)
            with dve.If(take_long_way(dve)):
                for n in range(F_AHEAD):
                    f_float(n)
                    f_low(n)
                for j in range(HT):
                    hid_value(j, long)
                    for n in f_turn(j):
                        f_float(n)
                        f_low(n)
                outputs(long)

        def self_attention_and_ffn_pe(pe, transpose_tokens, split_product):
            for k in range(2 * TT):
                q, t = divmod(k, TT)
                f = FRONT_BACK + k
                if t == 0:
                    pe.wait_ge(outs_added, (q + 1) * NCH * GP)
                pe.wait_ge(front_free, f - 3)
                for g in range(4):
                    last = nc.tensor.transpose(ps[:, f % 4, g * P:(g + 1) * P], att[:, 4 * q + g, t * P:(t + 1) * P],
                                               ident[:, :])
                last.then_inc(front_ready, 1)
            transpose_tokens(0, FRONT_LN2, norm_b, 1)
            def projection_item(n, i, bank):
                k, c = divmod(n, DC)
                if k:
                    left = [lambda d, v=v: v[:, d, c * P:(c + 1) * P] for v in wqkv[k]]
                    right = [lambda d, v=v: v[:, d, :] for v in xb_hl]
                else:
                    t, h = divmod(c, 2)
                    left = [lambda d, v=v: v[:, d, t * P:(t + 1) * P] for v in xb_hl]
                    right = [lambda d, v=v: v[:, d, 512 * h:512 * h + 512] for v in wqkv[0]]
                ins = split_product(ps[:, bank, :], left, right, i, i == 3 * DC - 1)
                if i == 3 * DC - 1:
                    ins.then_inc(work_ready, 1)

            for n in range(SA_FIRST):
                pe.wait_ge(work_out, W1 + n - 1)
                if n % DC == 0:
                    pe.wait_ge(w_split, W_SA + (n // DC + 1) * DC)
                if n < 2 * TT and n % 2 == 0:
                    pe.wait_ge(front_free, FRONT_LN2 + n + 2)
                for i in range(3 * DC):
                    projection_item(n, i, WORK + n % 2)
                if n % 2 == 0 and n // 2 + 1 < TT:
                    transpose_tokens(n // 2 + 1, FRONT_LN2, norm_b, 1)

            for k in range(SA_UNITS + SA_LAG + 3):
                if k < SA_UNITS:
                    h, t = divmod(k, TT)
                    if k % 8 == 0:
                        pe.wait_ge(work_out, W1 + SA_FIRST + k // 8)
                    at_least(pe, sa_exp, k - SA_BANKS + 1)
                    rows = slice(64 * (h % 2), 64 * (h % 2) + 64)
                    nc.tensor.matmul(ps[:, k % SA_BANKS, 0:(t + 1) * P], q2T[rows, h // 2, t * P:(t + 1) * P],
                                     k2T[rows, h // 2, 0:(t + 1) * P], start=True, stop=True).then_inc(sa_scores, 1)
                    if k // 8 + 1 < DC:
                        for i in range(k % 8 * Q_PER_UNIT, min(3 * DC, (k % 8 + 1) * Q_PER_UNIT)):
                            projection_item(SA_FIRST + k // 8, i, SA_BANKS)
                m = k - SA_LAG
                if 0 <= m < SA_UNITS:
                    t = m % TT
                    pe.wait_ge(sa_norm, m + 1)
                    at_least(pe, sa_turned_out, m - 1)
                    for c in range(t + 1):
                        last = nc.tensor.transpose(ps[:, WORK + m % 2, c * P:(c + 1) * P], sa_p[m % 4][:, c * P:(c + 1) * P],
                                                   ident[:, :])
                    last.then_inc(sa_turned, 1)
                m -= 2
                if m >= 0 and m % TT == TT - 1:
                    h = m // TT
                    pe.wait_ge(sa_turned_out, m + 1)
                    if h % 2 == 0:
                        at_least(pe, sa_out_split, h // 2 - 1)
                    for c in range(TT):
                        last = nc.tensor.matmul(ps[64 * (h % 2):64 * (h % 2) + 64, OUTS + h // 2 % 2, c * P:N],
                                                v2[:, c, h * DH2:(h + 1) * DH2], sa_pT[h % 2][:, c, c * P:N],
                                                start=(c == 0), stop=(c == TT - 1))
                    last.then_inc(sa_pv, 1)

            pe.wait_ge(w_split, len(w_jobs))
            pe.wait_ge(sa_out_split, H2 // 2)
            for k in range(2 * TT):
                t, h = divmod(k, 2)
                at_least(pe, proj_added, k - 1)
                left = [lambda d, v=v: v[:, d, t * P:(t + 1) * P] for v in sa_out]
                right = [lambda d, v=v: v[:, d, 512 * h:512 * h + 512] for v in wproj]
                for i in range(3 * DC):
                    last = split_product(ps[:, WORK + k % 2, :], left, right, i, i == 3 * DC - 1)
                last.then_inc(proj_ready, 1)
                if t >= 1 and h == 0:
                    transpose_tokens(t - 1, FRONT_LN3, norm_b, 2)

            def gate_up_product(j, m, way, c0, c1):
                left = [lambda d, v=v: v[:, d, :] for v in ring[j % 4][m]]
                right = [lambda d, v=v: v[:, d, c0:c1] for v in xb_hl]
                terms = ((0, 0), (0, 1)) if way is short else SPLIT_TERMS
                count = len(terms) * DC
                for i in range(count):
                    last = split_product(ps[:, (WORK, OUTS)[j % 2] + m, c0:c1], left, right, i, i == count - 1, terms)
                return last

            pe.wait_ge(front_free, FRONT_LN3 + 2 * (TT - 1))
            pe.wait_ge(short.hi, f_no["up", 0] + 1)
            pe.wait_ge(proj_added, 2 * TT)
            for m in range(2):
                gate_up_product(0, m, short, 0, N - P)
            transpose_tokens(TT - 1, FRONT_LN3, norm_b, 2)
            pe.wait_ge(front_free, FRONT_LN3 + 2 * TT)
            def gate_up(way):
                for j in range(HT):
                    pe.wait_ge(way.hi if way is short else way.split, f_no["up", j] + 1)
                    for m in range(2):
                        at_least(pe, (way.silu_ready, way.hid_ready)[m], j - 1)
                        from_token = N - P if j == 0 and way is short else 0
                        last = gate_up_product(j, m, way, from_token, N)
                        last.then_inc(way.gu_ready, 1)

            def down(way):
                for k in range(2 * TT):
                    t, h = divmod(k, 2)
                    at_least(pe, way.down_out, k - 3)
                    left = [lambda j, v=v: hid[j][v][:, 0, t * P:(t + 1) * P] for v in range(2)]
                    right = [lambda j, v=v: w_down[j][v][:, 0, 512 * h:512 * h + 512] for v in range(2)]
                    terms = ((0, 0), (1, 0)) if way is short else SPLIT_TERMS
                    count = len(terms) * HT
                    for i in range(count):
                        if k == 0 and i == count - 2 * len(terms):
                            pe.wait_ge(way.hid_split, HT)
                        last = split_product(ps[:, k % 4, :], left, right, i, i == count - 1, terms)
                    last.then_inc(way.down_ready, 1)
                    if way is short and k == 0:
                        pe.wait_ge(codes_checked, len(f_jobs) + 1)
                        pe.wait_ge(short.silu_ready, HT - 1)
                        nc.tensor.transpose(ps[0:1, WORK, 0:P], row_max[:, 0:1], ident[:, :]).then_inc(checks_turned, 1)

            gate_up(short)
            pe.wait_ge(short.hi, len(f_jobs))
            pe.wait_ge(short.hid_split, HT - 2)
            down(short)
            with pe.If(take_long_way(pe)):
                gate_up(long)
                pe.wait_ge(long.split, len(f_jobs))
                pe.wait_ge(long.hid_split, HT - 2)
                down(long)

        block = stack.enter_context(nc.Block())

        @block.sync
        def _(sp):
            for t in range(TT):
                sp.dma_start(x_a[:, t], x_v[t]).then_inc(x_loaded[t], 16)

            def load_w(j):
                src, _, _, slot = w_jobs[j]
                if slot_before[j] is not None:
                    sp.wait_ge(w_split, slot_before[j] + 1)
                sp.dma_start(slots[slot], src).then_inc(w_loaded[slot], 16)

            def load_ctx(c, chunk):
                at_least(sp, ctx_split, c)
                sp.dma_start(region(120, 8), ctx_v[bass.ds(chunk, 1)].rearrange("c p x -> (c p) x"))\
                    .then_inc(ctx_loaded, 16)

            for j in range(W_KV):
                load_w(j)
            load_ctx(0, 0)
            for j in range(W_KV, W_KV2):
                load_w(j)
            load_ctx(1, 1)
            for j in range(W_KV2, W_END):
                load_w(j)
            load_ctx(2, 2)
            with sp.Fori(0, NCH - 3) as i:
                load_ctx(i + 3, i + 3)
            for k in range(3):
                load_ctx(NCH + k, k)
            sp.wait_ge(scores_ready, NCH * UNITS)
            load_w(W_END)
            load_w(W_END + 1)
            load_ctx(NCH + 3, 3)
            for j in range(W_END + 2, W_SA + DC):
                load_w(j)
            sp.wait_ge(w_split, W_SA + DC)
            sp.dma_start(x1, x.rearrange("(t p) c -> p t c", p=P)).then_inc(x_again, 16)
            with sp.Fori(0, NCH - 4) as i:
                load_ctx(i + (NCH + 4), i + 4)
            self_attention_and_ffn_sp(sp, load_w)

        @block.gpsimd
        def _(pool):
            nc.gpsimd.memset(ident[:, :], 0.0).then_inc(ident_ready, 1)
            nc.gpsimd.memset(ident16[:, :], 0.0).then_inc(ident_ready, 1)
            nc.gpsimd.memset(ones[:, :], 1.0).then_inc(ident_ready, 1)
            pool.wait_ge(ident_ready, 3)
            for m in (ident, ident16):
                nc.gpsimd.affine_select(out=m[:, :], in_=m[:, :], compare_op=ALU.not_equal, fill=1.0, base=0,
                                        pattern=[[-1, P]], channel_multiplier=1).then_inc(ident_ready, 1)

            def key_tile(c, t):
                n = c * MT + t
                pool.wait_ge(work_out, key_no(c, t) + 1)
                nc.gpsimd.tensor_tensor(keys_sq[t], keys[t], keys[t], ALU.mult).then_inc(key_sq_ready, 1)
                pool.wait_ge(key_rs_ready, n + 1)
                nc.gpsimd.tensor_tensor(keys[t], keys[t], rs_key[t][:, :].unsqueeze(2).to_broadcast([P, HP, DH1]),
                                        ALU.mult).then_inc(key_normed, 1)
                pool.wait_ge(key_hi, n + 1)
                nc.gpsimd.tensor_tensor(key_stack[t][:, :, 1::2, :],
                                        keys[t].unsqueeze(2).to_broadcast([P, HP, 2, DH1]),
                                        key_stack[t][:, :, 0::2, :], ALU.subtract).then_inc(key_stacked, 1)

            def stage(s, b, p):
                if not (isinstance(s, int) and s + 1 >= STAGES):
                    for t in range(MT):
                        key_tile(s + 1, t)

            for t in range(TT):
                raw = q_raw[t % 2]
                pool.wait_ge(work_out, work_no["q", t, 1] + 1)
                nc.gpsimd.tensor_tensor(q_sq, raw, raw, ALU.mult).then_inc(q_sq_ready, 1)
                pool.wait_ge(q_rs_ready, t + 1)
                nc.gpsimd.tensor_tensor(raw, raw, rs_q[:, :].unsqueeze(2).to_broadcast([P, H1, DH1]),
                                        ALU.mult).then_inc(q_normed, 1)
            for t in range(MT):
                key_tile(0, t)
            stages(pool, stage)
            self_attention_and_ffn_pool(pool)

        @block.scalar
        def _(act):
            def split_w(j):
                src, hi, _, slot = w_jobs[j]
                act.wait_ge(w_loaded[slot], 16 * (slot_use[j] + 1))
                nc.scalar.activation(hi, slots[slot], ACT.Copy, scale=W_SCALE).then_inc(w_hi_ready, 1)

            def ln_hi(t, q, front, ln, hi):
                act.wait_ge(front_ready, front + 1)
                nc.scalar.activation(hi[:, 4 * q:4 * q + 4, t * P:(t + 1) * P],
                                     ps[:, front % 4, :].rearrange("p (d n) -> p d n", n=P), ACT.Copy,
                                     scale=ACT_SCALE).then_inc(ln_hi_ready, 1)

            def ctx_hi(c, b):
                act.wait_ge(ctx_loaded, (c + 1) * 16)
                nc.scalar.activation(ctx_hl[b][0], ctx_f, ACT.Copy, scale=ACT_SCALE).then_inc(ctx_hi_ready, 1)

            def copy_out(c, n, b):
                kind, t, h = TASKS[n]
                no = key_no(c, t) if kind == "K" else c * NT + (W0 + n)
                bank = WORK + TASK_BANK[n]
                act.wait_ge(work_ready, no + 1)
                if kind == "K":
                    at_least(act, key_stacked, c * MT + (t - 1))
                    nc.scalar.activation(keys[t], ps[:, bank, :].rearrange("p (h d) -> p h d", d=DH1), ACT.Copy,
                                         scale=1.0 / PROD).then_inc(work_out, 1)
                elif kind == "V":
                    nc.scalar.activation(values[b][:, t], ps[:, bank, :], ACT.Copy,
                                         scale=1.0 / PROD).then_inc(work_out, 1)
                else:
                    nc.scalar.activation(kT[b][:, 8 * h:8 * h + 8, t * P:(t + 1) * P],
                                         ps[:, bank, :].bitcast(F16).rearrange("p (h m) -> p h m", m=P),
                                         ACT.Copy).then_inc(work_out, 1)

            def key_high(c, t):
                act.wait_ge(key_normed, c * MT + (t + 1))
                nc.scalar.activation(key_stack[t][:, :, 0::2, :], keys[t].unsqueeze(2).to_broadcast([P, HP, 2, DH1]),
                                     ACT.Copy).then_inc(key_hi, 1)

            def q_high(t):
                act.wait_ge(q_normed, t + 1)
                nc.scalar.activation(q_stack[t % 2][:, :, 0:2, :], q_raw[t % 2].unsqueeze(2).to_broadcast([P, H1, 2, DH1]),
                                     ACT.Copy).then_inc(q_hi, 1)

            def early_out(task):
                kind, t, h = task
                no = work_no[task]
                act.wait_ge(work_ready, no + 1)
                bank = ps[:, WORK + no % 2, :]
                if kind == "q":
                    if t >= 2 and h == 0:
                        act.wait_ge(q_stacked, t - 1)
                    nc.scalar.activation(q_raw[t % 2][:, 16 * h:16 * h + 16], bank.rearrange("p (h d) -> p h d", d=DH1),
                                         ACT.Copy, scale=1.0 / PROD).then_inc(work_out, 1)
                elif kind == "qt":
                    dst = qT[8 * h // HP][:, 8 * h % HP:8 * h % HP + 8, t * P:(t + 1) * P]
                    nc.scalar.activation(dst, bank.bitcast(F16).rearrange("p (h m) -> p h m", m=P),
                                         ACT.Copy).then_inc(work_out, 1)
                else:
                    copy_out(0, t, 0)

            split_w(W_Q)
            for q in range(2):
                ln_hi(0, q, FRONT_LN1 + q, 0, xa_hl[0])
            for j in range(W_Q + 1, W_KV):
                split_w(j)
            w_next = W_KV
            for t in range(TT):
                early_out(("q", t, 0))
                if t + 1 < TT:
                    for q in range(2):
                        ln_hi(t + 1, q, FRONT_LN1 + 2 * (t + 1) + q, 0, xa_hl[0])
                if t == 0:
                    act.wait_ge(w_split, W_KV)
                if t >= 2:
                    for h in range(H1 // 8):
                        early_out(("qt", t - 2, h))
                if t >= 1:
                    q_high(t - 1)
                early_out(("q", t, 1))
                for _ in range(EARLY_SPLITS[t]):
                    split_w(w_next)
                    w_next += 1
                if t in (0, 2):
                    ctx_hi(t // 2, t // 2)
            early_out(("key", 0, 0))
            for h in range(H1 // 8):
                early_out(("qt", TT - 2, h))
            q_high(TT - 1)
            early_out(("key", 1, 0))
            key_high(0, 0)
            for h in range(H1 // 8):
                early_out(("qt", TT - 1, h))
            for n in range(2, NT):
                copy_out(0, n, 0)
                if n == 3:
                    key_high(0, 1)
                if n >= 4:
                    split_w(w_next)
                    w_next += 1

            def denominators_out(p, g):
                act.wait_ge(den_ready, p * GP + g + 1)
                nc.scalar.activation(group_den(g), ps[:, OUTS + g % 2, :], ACT.Copy).then_inc(den_out, 1)

            def stage(s, b, p):
                project = not (isinstance(s, int) and s + 1 >= STAGES)
                for u in range(UNITS):
                    n = s * UNITS + u
                    if isinstance(s, int) and s == 0 and u == 0:
                        act.wait_ge(w_split, W_END)
                    act.wait_ge(scores_ready, n + 1)
                    at_least(act, pv_done, s * (UNITS // 2) + (u // 2 - 1))
                    at_least(act, probs_summed, n - 3)
                    nc.scalar.activation(probs[u % 4], ps[:, SCORES + 2 * (u % 2):SCORES + 2 * (u % 2) + 2, :]
                                         .rearrange("p a n -> p (a n)"), ACT.Exp,
                                         scale=DH1 ** -0.5 / ACT_SCALE ** 2).then_inc(probs_ready, 1)
                    if due := denominators_due(s, u, p):
                        denominators_out(*due)
                    if isinstance(s, int) and s in (NCH, NCH + 1) and u in W_STEPS:
                        split_w(W_SA + (s - NCH) * 4 + W_STEPS.index(u))
                    if not project:
                        continue
                    if u == 1 and not (isinstance(s, int) and s + 2 >= STAGES):
                        ctx_hi(s + 2, b)
                    for k in range(NT):
                        if task_end[k] == u:
                            copy_out(s + 1, k, 1 - b)
                    for t in range(MT):
                        if task_end[t] + 3 == u:
                            key_high(s + 1, t)

            stages(act, stage)
            denominators_out(PASSES - 1, GP - 2)
            denominators_out(PASSES - 1, GP - 1)
            self_attention_and_ffn_act(act, split_w, ln_hi)

        @block.vector
        def _(dve):
            step_no = [0]

            def step(ins):
                ins.then_inc(dve_step, 1)
                step_no[0] = step_no[0] + 1
                dve.wait_ge(dve_step, step_no[0])

            def rsqrt(v, cols, res):
                y, t = nt_y[:, 0:cols], nt_t[:, 0:cols]
                step(nc.vector.tensor_scalar(y.bitcast(I32), v.bitcast(I32), -0.5, RSQRT_MAGIC, ALU.mult, ALU.add))
                for k in range(NEWTON):
                    step(nc.vector.tensor_tensor(t, y, y, ALU.mult))
                    step(nc.vector.scalar_tensor_tensor(t, t, -0.5, v, ALU.mult, ALU.mult))
                    last = nc.vector.scalar_tensor_tensor(res if k == NEWTON - 1 else y, t, 1.5, y, ALU.add, ALU.mult)
                    if k < NEWTON - 1:
                        step(last)
                return last

            def split_w(j):
                src, hi, lo, slot = w_jobs[j]
                dve.wait_ge(w_hi_ready, j + 1)
                nc.vector.scalar_tensor_tensor(lo, slots[slot], W_SCALE, hi, ALU.mult, ALU.subtract).then_inc(w_split, 1)

            def ctx_lo(c, b):
                dve.wait_ge(ctx_hi_ready, c + 1)
                nc.vector.scalar_tensor_tensor(ctx_hl[b][1], ctx_f, ACT_SCALE, ctx_hl[b][0], ALU.mult,
                                               ALU.subtract).then_inc(ctx_split, 1)

            def ln_tile(t, ln, src, norm, front):
                for k in range(2):
                    step(nc.vector.bn_stats(bn[:, k, :], src[:, t, 512 * k:512 * k + 512]))
                step(nc.vector.bn_aggr(mv[:, t, :], bn[:, :, :]))
                step(nc.vector.tensor_scalar(nt_v[:, 0:1], mv[:, t, 1:2], 1e-5, None, ALU.add))
                step(rsqrt(nt_v[:, 0:1], 1, rs_ln[:, t:t + 1]))
                if t >= 2:
                    dve.wait_ge(front_ready, front + 2 * (t - 1))
                nc.vector.tensor_scalar(norm[t % 2], src[:, t], mv[:, t, 0:1], rs_ln[:, t:t + 1], ALU.subtract,
                                        ALU.mult).then_inc(normed, 1)

            def ln_lo(t, q, front, ln, hl):
                dve.wait_ge(ln_hi_ready, ln * 2 * TT + 2 * t + q + 1)
                at = (slice(None), slice(4 * q, 4 * q + 4), slice(t * P, (t + 1) * P))
                nc.vector.scalar_tensor_tensor(hl[1][at], ps[:, front % 4, :].rearrange("p (d n) -> p d n", n=P),
                                               ACT_SCALE, hl[0][at], ALU.mult, ALU.subtract).then_inc(front_free, 1)

            def ln_low(t, ln, hl, front):
                for q in range(2):
                    ln_lo(t, q, front + 2 * t + q, ln, hl)

            def key_stats(c, t):
                dve.wait_ge(key_sq_ready, c * MT + (t + 1))
                v = nt_v[:, 0:HP]
                step(nc.vector.reduce_sum(v, keys_sq[t], axis=AX_X))
                step(nc.vector.tensor_scalar(v, v, 1.0 / (DH1 * ACT_SCALE ** 2), 1e-6 / ACT_SCALE ** 2, ALU.mult, ALU.add))
                rsqrt(v, HP, rs_key[t][:, :]).then_inc(key_rs_ready, 1)

            def first_ln(t):
                dve.wait_ge(x_loaded[t], 16)
                ln_tile(t, 0, x_a, norm_a, FRONT_LN1)

            first_ln(0)
            split_w(W_Q)
            ln_low(0, 0, xa_hl, FRONT_LN1)
            for j in range(W_Q + 1, W_KV):
                split_w(j)
            first_ln(1)
            first_ln(2)
            ln_low(1, 0, xa_hl, FRONT_LN1)
            w_next = W_KV
            for t in range(TT):
                dve.wait_ge(q_sq_ready, t + 1)
                step(nc.vector.reduce_sum(nt_v[:, :], q_sq, axis=AX_X))
                step(nc.vector.tensor_scalar(nt_v[:, :], nt_v[:, :], 1.0 / (DH1 * ACT_SCALE ** 2), 1e-6 / ACT_SCALE ** 2,
                                             ALU.mult, ALU.add))
                if t >= 1:
                    dve.wait_ge(q_normed, t)
                rsqrt(nt_v[:, :], H1, rs_q[:, :]).then_inc(q_rs_ready, 1)
                if t + 3 < TT:
                    first_ln(t + 3)
                if t + 2 < TT:
                    ln_low(t + 2, 0, xa_hl, FRONT_LN1)
                for _ in range(EARLY_SPLITS[t]):
                    if t < TT - 1:
                        split_w(w_next)
                        w_next += 1
                if t in (0, 2):
                    ctx_lo(t // 2, t // 2)
                dve.wait_ge(q_hi, t + 1)
                nc.vector.tensor_tensor(q_stack[t % 2][:, :, 2:4, :],
                                        q_raw[t % 2].unsqueeze(2).to_broadcast([P, H1, 2, DH1]),
                                        q_stack[t % 2][:, :, 0:2, :], ALU.subtract).then_inc(q_stacked, 1)
            key_stats(0, 0)
            for _ in range(EARLY_SPLITS[TT - 1]):
                split_w(w_next)
                w_next += 1
            key_stats(0, 1)
            while w_next < W_END:
                split_w(w_next)
                w_next += 1
            steps0 = step_no[0]
            STEPS = MT * (3 + 3 * NEWTON - 1)

            def add_outs(count, p, g, bank, first):
                at_least(dve, pv_done, (count + 1) * MT)
                at_least(dve, outs_added, count)
                if first:
                    ins = nc.vector.tensor_copy(att[:, p * GP + g], ps[:, bank, :])
                else:
                    ins = nc.vector.tensor_tensor(att[:, p * GP + g], ps[:, bank, :], att[:, p * GP + g], ALU.add)
                ins.then_inc(outs_added, 1)

            def invert(p, g):
                n = p * GP + g
                dve.wait_ge(den_turned, n + 1)
                nc.vector.reciprocal(rden[:, p, :, 4 * g:4 * g + 4],
                                     ps[:, OUTS + g % 2, :].rearrange("p (t j c) -> p t j c", j=4, c=DH1)[:, :, :, 0])\
                    .then_inc(den_inverted, 1)

            def stage(s, b, p):
                project = not (isinstance(s, int) and s + 1 >= STAGES)
                step_no[0] = s * STEPS + steps0
                first = first_of_pass(s)
                second = isinstance(s, int) and s % NCH == 1
                for u in range(UNITS):
                    g, t, head = unit(u)
                    n = s * UNITS + u
                    if u >= 2 and (due := denominators_due(s, u - 2, p)):
                        invert(*due)
                    dve.wait_ge(probs_ready, n + 1)
                    at_least(dve, probs_summed, n - 1)
                    acc = prob_sum[:, head * N:(head + 2) * N]
                    if first and t == 0:
                        ins = nc.vector.tensor_copy(acc, probs[u % 4])
                    else:
                        ins = nc.vector.tensor_tensor(acc, acc, probs[u % 4], ALU.add)
                    ins.then_inc(probs_summed, 1)
                    if u % 4 == 1 and not (p == 0 and first and u == 1):
                        g = (u - 2) // 4 % GP
                        add_outs(s * GP + (u - 2) // 4, p - 1 if first and u == 1 else p, g, OUTS + g % 2, (first and u > 1) or (second and u == 1))
                    if isinstance(s, int) and s in (NCH, NCH + 1) and u in W_STEPS:
                        split_w(W_SA + (s - NCH) * 4 + W_STEPS.index(u))
                    if not project:
                        continue
                    if u == 2 and not (isinstance(s, int) and s + 2 >= STAGES):
                        ctx_lo(s + 2, b)
                    for t in range(MT):
                        if task_end[t] + 1 == u:
                            key_stats(s + 1, t)
            stages(dve, stage)
            add_outs(STAGES * GP - 1, PASSES - 1, GP - 1, OUTS + (GP - 1) % 2, False)
            invert(PASSES - 1, GP - 2)
            invert(PASSES - 1, GP - 1)
            self_attention_and_ffn_dve(dve, step, split_w, ln_tile, ln_low)

        @block.tensor
        def _(pe):
            def transpose_tokens(t, front0, norm, ln):
                pe.wait_ge(normed, ln * TT + t + 1)
                for q in range(2):
                    f = front0 + 2 * t + q
                    at_least(pe, front_free, f - 3)
                    for k in range(4):
                        d = 4 * q + k
                        last = nc.tensor.transpose(ps[:, f % 4, k * P:(k + 1) * P], norm[t % 2][:, d * P:(d + 1) * P],
                                                   ident[:, :])
                    last.then_inc(front_ready, 1)

            def split_product(dst, left, right, i, last_item, terms=SPLIT_TERMS):
                d, k = divmod(i, len(terms))
                a, b_ = terms[k]
                return nc.tensor.matmul(dst, left[a](d), right[b_](d), start=(i == 0), stop=last_item)

            pe.wait_ge(ident_ready, 5)
            transpose_tokens(0, FRONT_LN1, norm_a, 0)
            for task in early:
                kind, t, h = task
                no = work_no[task]
                at_least(pe, work_out, no - 1)
                if kind == "q":
                    if h == 0:
                        pe.wait_ge(front_free, FRONT_LN1 + 2 * (t + 1))
                    left = [lambda d, v=v: v[:, d, t * P:(t + 1) * P] for v in xa_hl]
                    right = [lambda d, v=v: v[:, d, 512 * h:512 * h + 512] for v in wq]
                    for i in range(3 * DC):
                        if no == 0 and i % 3 == 0:
                            pe.wait_ge(w_split, W_Q + i // 3 + 1)
                        last = split_product(ps[:, WORK + no % 2, :], left, right, i, i == 3 * DC - 1)
                elif kind == "qt":
                    if h == 0:
                        pe.wait_ge(q_stacked, t + 1)
                    for k in range(8):
                        last = nc.tensor.transpose(ps[:, WORK + no % 2, :].bitcast(F16)[:, k * P:(k + 1) * P],
                                                   q_stack[t % 2][:, 8 * h + k].rearrange("p s d -> p (s d)"), ident16[:, :])
                else:
                    if t == 0:
                        pe.wait_ge(w_split, W_KV2)
                        pe.wait_ge(ctx_split, 1)
                    left = [lambda d, v=v: v[:, d, t * P:(t + 1) * P] for v in ctx_hl[0]]
                    right = [lambda d, v=v: v[:, d, 0:KW] for v in wkv[0]]
                    for i in range(3 * DC):
                        last = split_product(ps[:, WORK + no % 2, :], left, right, i, i == 3 * DC - 1)
                last.then_inc(work_ready, 1)
                if kind == "q" and h == 0 and t + 1 < TT:
                    transpose_tokens(t + 1, FRONT_LN1, norm_a, 0)

            def chunk_item(c, b, p, item):
                n, i, ends = item
                kind, t, h = TASKS[n]
                bank = ps[:, WORK + TASK_BANK[n], :]
                if i == 0:
                    pe.wait_ge(work_out, c * NT + (W0 + TASK_FREE[n]))
                    if n == 0:
                        pe.wait_ge(ctx_split, c + 1)
                    if kind == "T" and h == 0:
                        pe.wait_ge(key_stacked, c * MT + (t + 1))
                if kind == "T":
                    ins = nc.tensor.transpose(bank.bitcast(F16)[:, i * P:(i + 1) * P],
                                              key_stack[t][:, 8 * h + i].rearrange("p s d -> p (s d)"), ident16[:, :])
                else:
                    w0 = 0 if kind == "K" else KW
                    left = [lambda d, v=v: v[:, d, t * P:(t + 1) * P] for v in ctx_hl[b]]
                    right = [lambda d, v=v: v[:, d, w0:w0 + KW] for v in wkv[p]]
                    ins = split_product(bank, left, right, i, ends)
                if ends:
                    ins.then_inc(work_ready, 1)

            def times_values(q, b, count, divided=0):
                g, t, head = unit(2 * q)
                if t == 0:
                    at_least(pe, outs_added, count - 1)
                    if divided:
                        pe.wait_ge(den_inverted, divided)
                for j in range(4):
                    last = nc.tensor.matmul(ps[32 * j:32 * j + 32, OUTS + g % 2, :],
                                            values[b][:, t, (head + j) * DH1:(head + j + 1) * DH1],
                                            probs[(2 * q + j // 2) % 4][:, j % 2 * N:(j % 2 + 1) * N],
                                            start=(t == 0), stop=(t == MT - 1))
                last.then_inc(pv_done, 1)

            def denominators(p, g):
                done = (p + 1) * NCH
                pe.wait_ge(probs_summed, done * UNITS - UNITS + 4 * g + 4)
                pe.wait_ge(outs_added, done * GP - GP + g + 1)
                for j in range(4):
                    head = 4 * g + j
                    last = nc.tensor.matmul(ps[32 * j:32 * j + 32, OUTS + g % 2, :], ones[:, :],
                                            prob_sum[:, head * N:(head + 1) * N], start=True, stop=True)
                last.then_inc(den_ready, 1)

            def turn_denominators(p, g):
                pe.wait_ge(den_out, p * GP + g + 1)
                for t in range(TT):
                    last = nc.tensor.transpose(ps[:, OUTS + g % 2, t * P:(t + 1) * P], group_den(g)[:, t * P:(t + 1) * P],
                                               ident[:, :])
                last.then_inc(den_turned, 1)

            for its in per_step:
                for it in its:
                    if TASKS[it[0]][0] != "K":
                        chunk_item(0, 0, 0, it)

            def stage(s, b, p):
                project = not (isinstance(s, int) and s + 1 >= STAGES)
                for u in range(UNITS):
                    g, t, head = unit(u)
                    n = s * UNITS + u
                    if u == 0:
                        pe.wait_ge(work_out, s * NT + (W0 + 4))
                    if u == 2:
                        pe.wait_ge(work_out, s * NT + (W0 + 7))
                    if u == 5:
                        pe.wait_ge(work_out, s * NT + (W0 + 8))
                    at_least(pe, probs_ready, n - 1)
                    for k in range(2):
                        last = nc.tensor.matmul(ps[:, SCORES + 2 * (u % 2) + k, :],
                                                kT[b][:, head + k, t * P:(t + 1) * P], qT[p][:, head + k, :],
                                                start=True, stop=True)
                    last.then_inc(scores_ready, 1)
                    if u % 2 and u >= 3:
                        g = (u - 3) // 4
                        divided = p * GP + g - 1 if last_of_pass(s) and g >= 2 or first_of_pass(s) and p and g < 2 else 0
                        times_values((u - 3) // 2, b, s * GP + g, divided)
                    elif u == 1 and not (p == 0 and first_of_pass(s)):
                        times_values(UNITS // 2 - 1, 1 - b, s * GP - 1)
                    if due := denominators_due(s, u, p):
                        denominators(*due)
                    if u >= 1 and (due := denominators_due(s, u - 1, p)):
                        turn_denominators(*due)
                    if project:
                        if u == 0 and last_of_pass(s):
                            pe.wait_ge(w_split, W_END)
                        for it in per_step[u]:
                            chunk_item(s + 1, 1 - b, pass_of_next(s, p), it)
            stages(pe, stage)
            pe.wait_ge(probs_ready, STAGES * UNITS)
            times_values(UNITS // 2 - 1, 1, STAGES * GP - 1)
            for g in (GP - 2, GP - 1):
                denominators(PASSES - 1, g)
            for g in (GP - 2, GP - 1):
                turn_denominators(PASSES - 1, g)
            self_attention_and_ffn_pe(pe, transpose_tokens, split_product)


def laid_out(inputs):
    import numpy as np

    def tiles(w, cols):
        d, c = w.shape
        return w.reshape(d // 128, 128, c // cols, cols).transpose(2, 1, 0, 3)

    a = {k: np.asarray(v) for k, v in inputs.items()}
    wkv = np.concatenate([a["L0_xattn_Wk"], a["L0_xattn_Wv"]], 0)
    wkv = wkv.reshape(2, 512, 2, wkv.shape[1]).transpose(3, 0, 2, 1)
    return {
        "x": a["x"][0],
        "ctx_t": tiles(a["ctx_2048"][0].T, 256),
        "wq_t": a["L0_xattn_Wq"].T,
        "wkv_t": wkv.reshape(wkv.shape[0], -1),
        "wqkv_t": a["L0_attn_Wqkv"].T,
        "wproj_t": a["L0_attn_Wproj"].T,
        "wg_t": tiles(a["L0_ffn_wq_gate"].T, 128),
        "wu_t": tiles(a["L0_ffn_wq_up"].T, 128),
        "wd_t": a["L0_ffn_wq_down"].T,
        "s_gate": a["L0_ffn_s_gate"].reshape(-1, 128).T,
        "s_up": a["L0_ffn_s_up"].reshape(-1, 128).T,
        "s_down": a["L0_ffn_s_down"].reshape(1, -1),
    }


def kernel(**inputs):
    import numpy as np
    import concourse.bacc as bacc
    from concourse import mybir as mb
    from concourse.bass_utils import run_bass_kernel_spmd

    nc = bacc.Bacc("TRN2", target_bir_lowering=False, num_devices=1, dynamic_dma_scratch_size=1024)
    arrays, args = {}, []
    for name, a in laid_out(inputs).items():
        a = np.ascontiguousarray(a)
        arrays["in_" + name] = a
        args.append(nc.dram_tensor("in_" + name, a.shape, mb.dt.from_np(a.dtype), kind="ExternalInput").ap())
    shape = tuple(np.asarray(inputs["x"]).shape)
    args.append(nc.dram_tensor("out_0", shape[1:], mb.dt.float32, kind="ExternalOutput").ap())
    build_perceiver(nc, *args)
    r = run_bass_kernel_spmd(nc, [arrays], core_ids=[0])
    return np.asarray(r.results[0]["out_0"]).reshape(shape)
```
